# Optimizing a Trainium2 kernel written in Bass

```python
import numpy as np
import jax
import jax.numpy as jnp

def _softmax(x, axis=-1):
    return jax.nn.softmax(x, axis=axis)

def _gelu(x):
    return jax.nn.gelu(x, approximate=True)

def _silu(x):
    return jax.nn.silu(x)

def _sigmoid(x):
    return jax.nn.sigmoid(x)

def _layernorm(x, axis=-1, eps=1e-05):
    m = jnp.mean(x, axis=axis, keepdims=True)
    v = jnp.var(x, axis=axis, keepdims=True)
    return (x - m) / jnp.sqrt(v + eps)

def _scatter_add(tgt, idx, src, axis=0):
    return tgt.at[idx].add(src)

def _segment_sum(src, seg, n):
    return jax.ops.segment_sum(src, seg, n)
kernel_name = 'mk_recurrent_d1_jaxref_r8_f726b4'

def setup_inputs(seed: int=0):
    np.random.seed(seed)
    _w = jnp.asarray

    def _L0_attn_setup():
        import jax, jax.numpy as jnp
        import numpy as np
        D_MODEL = 128
        NUM_HEADS = 16
        D_K = D_MODEL // NUM_HEADS
        B, S = (4, 256)
        key = jax.random.key(seed)
        k1, k2, k3 = jax.random.split(key, 3)
        x = jax.random.normal(k1, (B, S, D_MODEL), dtype=jnp.float32)
        w_qkv = jax.random.normal(k2, (3, NUM_HEADS, D_K, D_MODEL), dtype=jnp.float32) / np.sqrt(D_MODEL)
        w_o = jax.random.normal(k3, (D_MODEL, D_MODEL), dtype=jnp.float32) / np.sqrt(D_MODEL)
        return {'x': x, 'w_qkv': w_qkv, 'w_o': w_o}
    _L0_attn_in = _L0_attn_setup()

    def _L0_ffn_setup():
        import jax, jax.numpy as jnp
        import numpy as np
        JITTER_EPS = 0.01

        def phi_routing(logits, jitter_eps=JITTER_EPS):
            m, sel = jax.lax.top_k(logits, 2)
            T, E = logits.shape
            m1 = m[:, :1]
            factor1 = jnp.maximum(jnp.abs(logits), m1)
            mask1 = (m1 - logits) / factor1 > 2.0 * jitter_eps
            p1 = jax.nn.softmax(jnp.where(mask1, -jnp.inf, logits), axis=-1)
            mult1 = jnp.take_along_axis(p1, sel[:, :1], axis=-1)
            m2 = m[:, 1:2]
            factor2 = jnp.maximum(jnp.abs(logits), m2)
            mask2 = (m2 - logits) / factor2 > 2.0 * jitter_eps
            drop_top1 = jnp.arange(E)[None, :] == sel[:, :1]
            p2 = jax.nn.softmax(jnp.where(mask2 | drop_top1, -jnp.inf, logits), axis=-1)
            mult2 = jnp.take_along_axis(p2, sel[:, 1:2], axis=-1)
            return (jnp.concatenate([mult1, mult2], axis=-1), sel)
        key = jax.random.key(seed)
        k = jax.random.split(key, 5)
        B, S, H, F, E = (1, 64, 128, 512, 8)
        return {'hidden_states': jax.random.normal(k[0], (B, S, H), jnp.float32), 'gate_w': jax.random.normal(k[1], (E, H), jnp.float32) * 0.02, 'w1': jax.random.normal(k[2], (E, F, H), jnp.float32) * 0.02, 'w2': jax.random.normal(k[3], (E, H, F), jnp.float32) * 0.02, 'w3': jax.random.normal(k[4], (E, F, H), jnp.float32) * 0.02}
    _L0_ffn_in = _L0_ffn_setup()
    _d = {'L0_attn_x': _L0_attn_in['x'], 'L0_attn_w_qkv': _L0_attn_in['w_qkv'], 'L0_attn_w_o': _L0_attn_in['w_o'], 'L0_ffn_gate_w': _L0_ffn_in['gate_w'], 'L0_ffn_w1': _L0_ffn_in['w1'], 'L0_ffn_w2': _L0_ffn_in['w2'], 'L0_ffn_w3': _L0_ffn_in['w3']}
    _x0 = _d['L0_attn_x']
    _d['L0_attn_x'] = jax.random.normal(jax.random.fold_in(jax.random.key(seed), 1), (1, 2048, 128), dtype=_x0.dtype)
    del _x0
    return _d

def reference(L0_attn_x, L0_attn_w_qkv, L0_attn_w_o, L0_ffn_gate_w, L0_ffn_w1, L0_ffn_w2, L0_ffn_w3):

    def _L0_attn_ref(x, w_qkv, w_o):
        import jax, jax.numpy as jnp
        import numpy as np
        D_MODEL = 128
        NUM_HEADS = 16
        D_K = D_MODEL // NUM_HEADS
        B, S = (4, 256)
        seq_len = x.shape[-2]
        d_k = w_qkv.shape[-2]
        qkv = jnp.einsum('bsm,qhkm->qbhsk', x, w_qkv)
        Q, K, V = (qkv[0], qkv[1], qkv[2])
        scores = jnp.einsum('bhsk,bhtk->bhst', Q, K) / jnp.sqrt(jnp.asarray(d_k, x.dtype))
        causal = jnp.tril(jnp.ones((seq_len, seq_len), dtype=bool))
        scores = jnp.where(causal, scores, -jnp.inf)
        probs = jax.nn.softmax(scores, axis=-1)
        attn = jnp.einsum('bhst,bhtk->bhsk', probs, V)
        b, h, s, k = attn.shape
        attn_cat = jnp.transpose(attn, (0, 2, 1, 3)).reshape(b, s, h * k)
        return jnp.einsum('bsd,md->bsm', attn_cat, w_o)

    def _L0_ffn_ref(hidden_states, gate_w, w1, w2, w3):
        import jax, jax.numpy as jnp
        import numpy as np
        JITTER_EPS = 0.01

        def phi_routing(logits, jitter_eps=JITTER_EPS):
            m, sel = jax.lax.top_k(logits, 2)
            T, E = logits.shape
            m1 = m[:, :1]
            factor1 = jnp.maximum(jnp.abs(logits), m1)
            mask1 = (m1 - logits) / factor1 > 2.0 * jitter_eps
            p1 = jax.nn.softmax(jnp.where(mask1, -jnp.inf, logits), axis=-1)
            mult1 = jnp.take_along_axis(p1, sel[:, :1], axis=-1)
            m2 = m[:, 1:2]
            factor2 = jnp.maximum(jnp.abs(logits), m2)
            mask2 = (m2 - logits) / factor2 > 2.0 * jitter_eps
            drop_top1 = jnp.arange(E)[None, :] == sel[:, :1]
            p2 = jax.nn.softmax(jnp.where(mask2 | drop_top1, -jnp.inf, logits), axis=-1)
            mult2 = jnp.take_along_axis(p2, sel[:, 1:2], axis=-1)
            return (jnp.concatenate([mult1, mult2], axis=-1), sel)
        B, S, H = hidden_states.shape
        E = w1.shape[0]
        x = hidden_states.reshape(-1, H)
        logits = x @ gate_w.T
        routing_weights, selected = phi_routing(logits)
        T = x.shape[0]
        wte = jnp.zeros((T, E), x.dtype).at[jnp.arange(T)[:, None], selected].add(routing_weights)
        out = jnp.zeros_like(x)
        for e in range(E):
            h = jax.nn.silu(x @ w1[e].T) * (x @ w3[e].T)
            out = out + wte[:, e:e + 1] * (h @ w2[e].T)
        return out.reshape(B, S, H)
    x = L0_attn_x
    xn = _layernorm(x, axis=-1)
    s = _L0_attn_ref(xn, L0_attn_w_qkv, L0_attn_w_o)
    g = _silu(_L0_ffn_ref(xn, L0_ffn_gate_w, L0_ffn_w1, L0_ffn_w2, L0_ffn_w3))
    x = x + s * g
    return x

_drawn_inputs = setup_inputs


def setup_inputs(seed=0):
    import zlib

    import numpy as np

    out = dict(_drawn_inputs(seed))
    spreads = {}
    factors = {'L0_attn_w_qkv': 8.0,
     'L0_attn_w_o': 8.0,
     'L0_ffn_gate_w': 8.0,
     'L0_ffn_w1': 8.0,
     'L0_ffn_w2': 8.0,
     'L0_ffn_w3': 8.0}
    for name, (base, spread) in spreads.items():
        noise = np.random.default_rng([zlib.crc32(name.encode()), seed]).standard_normal(out[name].shape)
        drawn = base * np.exp(spread * noise) if base else spread * noise
        out[name] = jnp.asarray(drawn.astype(out[name].dtype))
    for name, factor in factors.items():
        out[name] = (out[name] * factor).astype(out[name].dtype)
    return out
```

```python
from contextlib import ExitStack

import concourse.bass as bass
from concourse import mybir

F32 = mybir.dt.float32
BF16 = mybir.dt.bfloat16
U32 = mybir.dt.uint32
I32 = mybir.dt.int32
ALU = mybir.AluOpType
ACT = mybir.ActivationFunctionType
AX = mybir.AxisListType

P = 128
T = 2048
NT = T // P
D = 128
H = 16
DK = D // H
HG = 4
NG = H // HG
CW = 512
NC = T // CW
TC = CW // P
NPART = 3
SK = NPART * NPART * DK
SKM = SK + NPART
VW = 2 * DK
E = 8
F = 512
FC = F // P
MT = (2 * T + E * (P - 1)) // P
NEG = -3.0e38
EPS = 1e-5
JITTER2 = 2.0 * 0.01
SCALE = DK ** -0.5

UNITS = [(c, j) for c in range(NC) for j in range(TC * (c + 1))]
UNIT_AT = {u: q for q, u in enumerate(UNITS)}
NU = len(UNITS)
NPAIR = 2 * NU


def unit_columns(c, j):
    first = P * max(0, j - TC * c)
    return first, CW - first


def max_items():
    items, due = [], []
    for i in range(NT):
        for c in range(i // TC + 1):
            for h in range(HG):
                items.append(("block", i, c, h))
                if due and len(items) >= due[0][0]:
                    items.append(("turn", due.pop(0)[1]))
        if i % TC == TC - 1:
            due.append((len(items) + 7, i // TC))
    return items + [("turn", s) for _, s in due]


ITEMS = max_items()
NI = len(ITEMS)
TURN_AT = {it[1]: n for n, it in enumerate(ITEMS) if it[0] == "turn"}
LAST_BLOCK = {s: max(n for n, it in enumerate(ITEMS) if it[0] == "block" and it[1] // TC == s) for s in range(NC)}


def block_width(i, c):
    return CW if c < i // TC else P * (i % TC + 1)


def item_cost(it):
    return block_width(it[1], it[2]) + 60 if it[0] == "block" else 60


def max_share():
    total_u = sum(unit_columns(*u)[1] + 60 for u in UNITS)
    total_i = sum(item_cost(it) for it in ITEMS)
    share, n, done_u, done_i = [], 0, 0, 0
    for u in UNITS:
        done_u += unit_columns(*u)[1] + 60
        n0 = n
        while n < NI and done_i < total_i * done_u / total_u / 0.93:
            done_i += item_cost(ITEMS[n])
            n += 1
        share.append((n0, n))
    return share


SHARE = max_share()


def build(nc, x, wqkvT, woT, gateT, w1T, w3T, w2T, out):
    ctx = ExitStack()
    with ctx:
        def sb(name, shape, dt=F32):
            return ctx.enter_context(nc.sbuf_tensor(name, shape, dt))

        def sem(name):
            return ctx.enter_context(nc.semaphore(name))

        qparts = nc.dram_tensor("qparts", [NPART, DK, H, T], BF16, kind="Internal").ap()
        kparts = nc.dram_tensor("kparts", [NPART, DK, H, T], BF16, kind="Internal").ap()
        mparts = nc.dram_tensor("mparts", [NPART, H, T], BF16, kind="Internal").ap()
        vones = nc.dram_tensor("vones", [P, NT, H, VW], F32, kind="Internal").ap()
        attn_raw = nc.dram_tensor("attn_raw", [H, VW, T], F32, kind="Internal").ap()
        slot_x = nc.dram_tensor("slot_x", [MT * P, D], F32, kind="Internal").ap()
        slot_y = nc.dram_tensor("slot_y", [MT * P, D], F32, kind="Internal").ap()

        psS = ctx.enter_context(nc.psum_tensor("psS", [P, 4, CW], F32))
        psM = ctx.enter_context(nc.psum_tensor("psM", [P, 3, CW], F32))
        psO = ctx.enter_context(nc.psum_tensor("psO", [P, CW], F32))

        X = sb("X", [P, NT, D])
        xn = sb("xn", [P, NT, D])
        xnT = sb("xnT", [P, T])
        wqkv_sb = sb("wqkv_sb", [P, 3 * D])
        wo_sb = sb("wo_sb", [P, D])
        gate_sb = sb("gate_sb", [P, E])
        W1 = sb("W1", [P, E * F])
        W3 = sb("W3", [P, E * F])
        W2 = sb("W2", [P, E * FC * D])
        stats = sb("stats", [P, NT, 6])
        mv = sb("mv", [P, NT, 2])
        var_eps = sb("var_eps", [P, NT])
        minus_half = sb("minus_half", [P, TC])
        rstd = sb("rstd", [P, NT])
        ident = sb("ident", [P, P])
        identb = sb("identb", [P, P], BF16)
        behind = sb("behind", [P, P], BF16)
        before = sb("before", [P, P])
        ones = sb("ones", [P, P])
        causal = sb("causal", [P, CW])
        Vp = sb("Vp", [P, NT, H, VW])
        rest = sb("rest", [P, 2, CW])
        QA = sb("QA", [P, HG, T], BF16)
        KA = sb("KA", [P, HG, T], BF16)
        QB = sb("QB", [P, HG, T], BF16)
        KB = sb("KB", [P, HG, T], BF16)
        QP = QB[:, 0:NPART, :]
        KP = KB[:, 0:NPART, :]
        zeros = QA[:, :, :].rearrange("p h n -> p (h n)").bitcast(F32)[:, 0:MT * D // 3]
        VA = sb("VA", [P, NT, HG, VW])
        probs = sb("probs", [P, 2, HG, CW])
        junk = sb("junk", [P, 3, CW], BF16)
        mpart = sb("mpart", [P, HG, NT, NC])
        mfull = sb("mfull", [P, NC, HG * TC])
        mrest = sb("mrest", [P, NC, HG * TC])
        msplit = sb("msplit", [P, NC, NPART, HG * TC], BF16)
        mturn = sb("mturn", [NPART * HG * TC, NC, P], BF16)
        orow = xnT[:, :].rearrange("p (c n) -> p c n", c=NC)

        x_in = [sem(f"x_in{k}") for k in range(NC)]
        w_in = sem("w_in")
        ew_in = sem("ew_in")
        cst = sem("cst")
        dve_c = sem("dve_c")
        xn_ok = sem("xn_ok")
        var_ok = sem("var_ok")
        rstd_ok = sem("rstd_ok")
        xt_ps = sem("xt_ps")
        xt_ok = sem("xt_ok")
        lg_ps = sem("lg_ps")
        v_ps = sem("v_ps")
        v_ok = sem("v_ok")
        qk_ps = sem("qk_ps")
        p1_ok = sem("p1_ok")
        r1_ok = sem("r1_ok")
        p2_ok = sem("p2_ok")
        p3_ok = sem("p3_ok")
        parts_out = sem("parts_out")
        vones_out = sem("vones_out")
        kset = sem("kset")
        v_set = sem("v_set")
        o_zero = sem("o_zero")
        kb_in = [sem(f"kb_in{p}") for p in range(NC)]
        qb_in = [sem(f"qb_in{p}") for p in range(NC)]
        ka_in = [sem(f"ka_in{p}") for p in range(NC)]
        qa_in = [sem(f"qa_in{p}") for p in range(NC)]
        va_in = [sem(f"va_in{p}") for p in range(NC)]
        m_mm = sem("m_mm")
        m_red = sem("m_red")
        m_full = sem("m_full")
        m_cut = sem("m_cut")
        m_chain = sem("m_chain")
        m_out = sem("m_out")
        d_passed, p_passed, l_passed = sem("d_passed"), sem("p_passed"), sem("l_passed")
        s_mm = sem("s_mm")
        s_exp = sem("s_exp")
        o_mm = sem("o_mm")
        o_row = sem("o_row")
        o_out = sem("o_out")
        route = Route(nc, sb, sem, zeros)
        ffn = Ffn(nc, sb, sem, probs[:, :, :, :].rearrange("p b h n -> p (b h) n"))
        fin = Final(nc, sem, QB, KB, Vp)

        def group(g):
            return bass.ds(g * HG, HG)

        block = ctx.enter_context(nc.Block())

        @block.sync
        def _(sp):
            def load_k(dst, g, p, done):
                for i in range(NPART):
                    sp.dma_start(
                        dst[i * NPART * DK:(i + 1) * NPART * DK, :, p * CW:(p + 1) * CW],
                        kparts.rearrange("j k h n -> (j k) h n")[:, group(g), p * CW:(p + 1) * CW],
                    ).then_inc(done, 16)

            def load_q(dst, g, p, done):
                for i in range(NPART):
                    for j in range(NPART):
                        r = (i * NPART + j) * DK
                        sp.dma_start(dst[r:r + DK, :, p * CW:(p + 1) * CW],
                                     qparts[i, :, group(g), p * CW:(p + 1) * CW]).then_inc(done, 16)

            def load_m(g, p, done):
                sp.dma_start(QA[SK:SKM, :, p * CW:(p + 1) * CW],
                             mparts[:, group(g), p * CW:(p + 1) * CW]).then_inc(done, 16)

            def load_v(g, p):
                sp.dma_start(VA[:, p * TC:(p + 1) * TC, :, :].rearrange("p j h w -> p j (h w)"),
                             vones[:, p * TC:(p + 1) * TC, group(g), :].rearrange("p j h w -> p j (h w)")
                             ).then_inc(va_in[p], 16)

            def store_m(g, s):
                for a in range(NPART):
                    sp.dma_start(mparts[a, group(g), s * CW:(s + 1) * CW].rearrange("h (i n) -> h i n", n=P),
                                 mturn[a * HG * TC:(a + 1) * HG * TC, s, :]).then_inc(m_out, 16)

            orow4 = [orow[32 * h:32 * h + VW, :, :] for h in range(HG)]

            def store_o(g, c):
                for h in range(HG):
                    sp.dma_start(attn_raw[bass.ds(g * HG + h, 1), :, c * CW:(c + 1) * CW].rearrange("a w n -> (a w) n"),
                                 orow4[h][:, c, :]).then_inc(o_out, 16)

            sp.sem_inc(o_out, 1)
            for k in range(NC):
                sp.dma_start(X[:, TC * k:TC * (k + 1), :],
                             x[k * CW:(k + 1) * CW, :].rearrange("(i p) d -> p i d", p=P)).then_inc(x_in[k], 16)
            sp.wait_ge(route.zeroed, 1)
            for k in range(3):
                sp.dma_start(slot_x.rearrange("(p r) d -> p (r d)", p=P)[:, k * MT * D // 3:(k + 1) * MT * D // 3],
                             route.zeros[:, :]).then_inc(route.filled, 16)
            for k in range(NC):
                for w, (src, dst) in enumerate(((KP, kparts), (QP, qparts))):
                    sp.wait_ge(p3_ok, 2 * k + w + 1)
                    for i in range(NPART):
                        sp.dma_start(dst[i, :, :, k * CW:(k + 1) * CW].rearrange("k h n -> h k n"),
                                     src[:, i, k * CW:(k + 1) * CW]).then_inc(parts_out, 16)
            sp.wait_ge(v_ok, NC)
            sp.dma_start(vones, Vp[:, :, :, :]).then_inc(vones_out, 16)
            sp.wait_ge(parts_out, 16 * 2 * NC * NPART)
            for p in range(NC):
                load_k(KB, 0, p, kb_in[p])
                load_q(QB, 0, p, qb_in[p])
            sp.wait_ge(vones_out, 16)
            sp.wait_ge(route.filled, 48)
            sp.wait_ge(kset, 1)
            for p in range(NC):
                load_k(KA, 0, p, ka_in[p])
                load_q(QA, 0, p, qa_in[p])
                load_v(0, p)
            for s in range(NC):
                sp.wait_ge(m_red, TURN_AT[s] + 1)
                store_m(0, s)
                sp.wait_ge(m_mm, LAST_BLOCK[s] + 1)
                load_q(QB, 1, s, qb_in[s])
                sp.wait_ge(m_out, 16 * NPART * (s + 1))
                load_m(0, s, qa_in[s])
            for p in range(NC):
                load_k(KB, 1, p, kb_in[p])

            with sp.Fori(0, NG - 1) as g:
                nxt = (g + 2) % NG
                for c in range(NC):
                    if c == NC - 1:
                        for p in range(NC - 1):
                            q = UNIT_AT[(c, TC * p + TC - 1)]
                            sp.wait_ge(s_mm, NPAIR * g + 2 * q + 2)
                            load_k(KA, g + 1, p, ka_in[p])
                            sp.wait_ge(o_mm, NU * g + q + 1)
                            load_v(g + 1, p)
                    sp.wait_ge(m_red, NI * (g + 1) + TURN_AT[c] + 1)
                    store_m(g + 1, c)
                    sp.wait_ge(m_mm, NI * (g + 1) + LAST_BLOCK[c] + 1)
                    load_q(QB, nxt, c, qb_in[c])
                    if c == NC - 1:
                        for p in range(NC):
                            load_k(KB, nxt, p, kb_in[p])
                    q = UNIT_AT[(c, TC * c + TC - 1)]
                    sp.wait_ge(s_mm, NPAIR * g + 2 * q + 2)
                    if c == NC - 1:
                        load_k(KA, g + 1, c, ka_in[c])
                    load_q(QA, g + 1, c, qa_in[c])
                    sp.wait_ge(m_out, (16 * NPART * NC) * (g + 1) + 16 * NPART * (c + 1))
                    load_m(g + 1, c, qa_in[c])
                    sp.wait_ge(o_row, NC * g + c + 2)
                    store_o(g, c)
                    if c == NC - 1:
                        load_v(g + 1, c)

            ffn.sp(sp, slot_x, slot_y, route)

            for c in range(NC):
                sp.wait_ge(o_row, NC * (NG - 1) + c + 2)
                store_o(NG - 1, c)
            sp.wait_ge(o_out, 16 * H * NC + 1)
            fin.sp(sp, attn_raw, out)

        @block.gpsimd
        def _(pool):
            nc.gpsimd.memset(ident[:, :], 0.0).then_inc(cst, 1)
            nc.gpsimd.memset(ones[:, :], 1.0).then_inc(cst, 1)
            nc.gpsimd.memset(causal[:, :], 0.0).then_inc(cst, 1)
            nc.gpsimd.memset(minus_half[:, :], -0.5).then_inc(cst, 1)
            pool.wait_ge(cst, 4)
            nc.gpsimd.affine_select(out=ident[:, :], in_=ident[:, :], compare_op=ALU.not_equal, fill=1.0,
                                    base=0, pattern=[[-1, P]], channel_multiplier=1).then_inc(cst, 1)
            nc.gpsimd.affine_select(out=before[:, :], in_=ones[:, :], compare_op=ALU.is_gt, fill=0.0,
                                    base=0, pattern=[[1, P]], channel_multiplier=-1).then_inc(cst, 1)
            nc.gpsimd.affine_select(out=causal[:, CW - P:], in_=causal[:, CW - P:], compare_op=ALU.is_ge, fill=NEG,
                                    base=0, pattern=[[-1, P]], channel_multiplier=1).then_inc(cst, 1)
            pool.wait_ge(cst, 5)
            nc.gpsimd.tensor_copy(identb[:, :], ident[:, :]).then_inc(cst, 1)
            nc.gpsimd.memset(behind[:, :], 0.0).then_inc(cst, 1)
            pool.wait_ge(cst, 9)
            nc.gpsimd.affine_select(out=behind[:, :], in_=behind[:, :], compare_op=ALU.is_ge, fill=NEG,
                                    base=0, pattern=[[1, P]], channel_multiplier=-1).then_inc(cst, 1)
            for k in range(NC):
                pool.wait_ge(var_ok, k + 1)
                nc.gpsimd.tensor_tensor(rstd[:, TC * k:TC * k + TC], var_eps[:, TC * k:TC * k + TC],
                                        minus_half[:, 0:TC], ALU.pow).then_inc(rstd_ok, 1)
            route.pool_constants(pool)
            for n in range(2 * NC):
                dst = (KP, QP)[n % 2]
                pool.wait_ge(p2_ok, n + 1)
                cols = slice(n // 2 * CW, n // 2 * CW + CW)
                nc.gpsimd.tensor_tensor(dst[:, 2, cols], rest[:, n % 2, :], dst[:, 1, cols],
                                        ALU.subtract).then_inc(p3_ok, 1)
            pool.wait_ge(p3_ok, 2 * NC)
            nc.gpsimd.memset(KA[64:96, :, :], -1.0).then_inc(kset, 1)
            pool.wait_ge(kset, 1)

            def cut_maxima(gm, s):
                wait_apart(pool, m_full, gm * NC + s + 1, l_passed)
                nc.gpsimd.tensor_copy(msplit[:, s, 0, :], mfull[:, s, :]).then_inc(m_chain, 1)
                pool.wait_ge(m_chain, gm * (3 * NC) + 3 * s + 1)
                nc.gpsimd.tensor_tensor(mrest[:, s, :], mfull[:, s, :], msplit[:, s, 0, :],
                                        ALU.subtract).then_inc(m_chain, 1)
                wait_apart(pool, m_chain, gm * (3 * NC) + 3 * s + 2, l_passed)
                nc.gpsimd.tensor_copy(msplit[:, s, 1, :], mrest[:, s, :]).then_inc(m_chain, 1)
                pool.wait_ge(m_chain, gm * (3 * NC) + 3 * s + 3)
                nc.gpsimd.tensor_tensor(msplit[:, s, 2, :], mrest[:, s, :], msplit[:, s, 1, :],
                                        ALU.subtract).then_inc(m_cut, 1)

            route.pool_slots(pool)
            n = 0
            for s, upto in enumerate((4, 12, 22, 2 * NT)):
                while n < upto:
                    route.scatter(pool, xn, slot_x, n)
                    n += 1
                cut_maxima(0, s)

            with pool.Fori(0, NG - 1) as g:
                for s in range(NC):
                    cut_maxima(g + 1, s)
            ffn.pool(pool)
            for p in range(NC):
                pool.wait_ge(qb_in[p], 144 * (NG + 1))
                pool.wait_ge(kb_in[p], 48 * (NG + 1))
            for n in range(2 * NT):
                fin.gather(pool, route, slot_y, n)

        @block.scalar
        def _(act):
            act.sem_inc(o_row, 1)
            act.dma_start(wqkv_sb[:, :], wqkvT).then_inc(w_in, 16)
            act.dma_start(gate_sb[:, :], gateT).then_inc(w_in, 16)
            act.dma_start(wo_sb[:, :], woT).then_inc(w_in, 16)
            act.dma_start(W1[:, :].rearrange("p (e f) -> p e f", e=E), w1T.rearrange("e p f -> p e f")).then_inc(ew_in, 16)
            act.dma_start(W3[:, :].rearrange("p (e f) -> p e f", e=E), w3T.rearrange("e p f -> p e f")).then_inc(ew_in, 16)
            for e in range(E):
                act.dma_start(W2[:, e * FC * D:(e + 1) * FC * D].rearrange("p (c d) -> p c d", c=FC),
                              w2T[e].rearrange("(c p) d -> p c d", p=P)).then_inc(ew_in, 16)
            for k in range(NC):
                act.wait_ge(xt_ps, k + 1)
                nc.scalar.activation(xnT[:, k * CW:(k + 1) * CW], psS[:, k, :], ACT.Copy).then_inc(xt_ok, 1)
            act.wait_ge(v_set, 1)
            for n in range(2 * NC):
                dst = (KP, QP)[n % 2]
                cols = slice(n // 2 * CW, n // 2 * CW + CW)
                act.wait_ge(qk_ps, n + 1)
                nc.scalar.activation(dst[:, 0, cols], psM[:, n % 3, :], ACT.Copy).then_inc(p1_ok, 1)
                act.wait_ge(r1_ok, n + 1)
                nc.scalar.activation(dst[:, 1, cols], rest[:, n % 2, :], ACT.Copy).then_inc(p2_ok, 1)
                if n % 2:
                    k = n // 2
                    act.wait_ge(v_ps, k + 1)
                    nc.scalar.activation(Vp[:, k * TC:(k + 1) * TC, :, 0:DK],
                                         psS[:, k, :].rearrange("p (j h w) -> p j h w", j=TC, h=H),
                                         ACT.Copy).then_inc(v_ok, 1)
            route.act(act)

            def evacuate(g, c):
                act.wait_ge(o_mm, g * NU + UNIT_AT[(c, TC * c + TC - 1)] + 1)
                act.wait_ge(o_out, g * (16 * HG * NC) + 1)
                nc.scalar.activation(orow[:, c, :], psO[:, :], ACT.Copy).then_inc(o_row, 1)

            def exps(g):
                for q, (c, j) in enumerate(UNITS):
                    first, w = unit_columns(c, j)
                    for p in range(2):
                        act.wait_ge(s_mm, g * NPAIR + 2 * q + p + 1)
                        if p == 0 and q >= 2:
                            act.wait_ge(o_mm, g * NU + q - 1)
                        nc.scalar.activation(probs[:, q % 2, 2 * p:2 * p + 2, 0:w], psS[:, 2 * p:2 * p + 2, 0:w],
                                             ACT.Exp, scale=SCALE).then_inc(s_exp, 1)
                        if p == 0 and j == 0 and c > 0:
                            evacuate(g, c - 1)
                evacuate(g, NC - 1)

            with act.Fori(0, NG - 1) as g:
                exps(g)
            ffn.act(act, psS, psM)
            exps(NG - 1)
            fin.act(act)

        @block.vector
        def _(dve):
            chain = [0]

            def link(ins):
                chain[0] += 1
                ins.then_inc(dve_c, 1)
                dve.wait_ge(dve_c, chain[0])

            nc.vector.memset(mpart[:, :, :, :], NEG)
            nc.vector.memset(psO[:, :], 0.0).then_inc(o_zero, 1)
            nc.vector.memset(Vp[:, :, :, :], 1.0).then_inc(v_set, 1)
            for k in range(NC):
                dve.wait_ge(x_in[k], 16)
                for i in range(TC * k, TC * k + TC):
                    last = nc.vector.bn_stats(stats[:, i, :], X[:, i, :])
                link(last)
                for i in range(TC * k, TC * k + TC):
                    last = nc.vector.bn_aggr(mv[:, i, :], stats[:, i, :])
                link(last)
                nc.vector.tensor_scalar(var_eps[:, TC * k:TC * k + TC], mv[:, TC * k:TC * k + TC, 1], EPS, None,
                                        ALU.add).then_inc(var_ok, 1)
                dve.wait_ge(rstd_ok, k + 1)
                for i in range(TC * k, TC * k + TC):
                    last = nc.vector.tensor_scalar(xn[:, i, :], X[:, i, :], mv[:, i, 0:1], rstd[:, i:i + 1],
                                                   ALU.subtract, ALU.mult)
                last.then_inc(xn_ok, 1)
            for n in range(2 * NC):
                dst = (KP, QP)[n % 2]
                cols = slice(n // 2 * CW, n // 2 * CW + CW)
                dve.wait_ge(p1_ok, n + 1)
                if n >= 2:
                    dve.wait_ge(p3_ok, n - 1)
                nc.vector.tensor_tensor(rest[:, n % 2, :], psM[:, n % 3, :], dst[:, 0, cols],
                                        ALU.subtract).then_inc(r1_ok, 1)
            dve.wait_ge(lg_ps, 1)
            route.dve(dve, link, psO)

            def max_item(gm, n):
                it = ITEMS[n]
                if ITEMS[n][0] == "block" and ITEMS[n][2] == ITEMS[n][1] // TC:
                    wait_apart(dve, m_mm, gm * NI + n + 1, d_passed)
                else:
                    dve.wait_ge(m_mm, gm * NI + n + 1)
                if it[0] == "turn":
                    dve.wait_ge(m_out, gm * (16 * NPART * NC))
                    nc.vector.tensor_copy(mturn[:, it[1], :], psM[:, n % 3, :].bitcast(BF16)[0:NPART * HG * TC, 0:P]
                                          ).then_inc(m_red, 1)
                    return
                _, i, c, h = it
                w = block_width(i, c)
                if c < i // TC:
                    nc.vector.tensor_reduce(out=mpart[:, h, i, c:c + 1], in_=psM[:, n % 3, :], axis=AX.X,
                                            op=ALU.max).then_inc(m_red, 1)
                else:
                    nc.vector.tensor_tensor_reduce(
                        out=junk[:, n % 3, 0:w], in0=psM[:, n % 3, 0:w], in1=causal[:, CW - w:], scale=1.0, scalar=NEG,
                        op0=ALU.add, op1=ALU.max, accum_out=mpart[:, h, i, c:c + 1]).then_inc(m_red, 1)
                if n in LAST_BLOCK.values():
                    s = i // TC
                    dve.wait_ge(m_red, gm * NI + n + 1)
                    nc.vector.tensor_reduce(out=mfull[:, s, :].rearrange("p (h i) -> p h i", h=HG),
                                            in_=mpart[:, :, s * TC:(s + 1) * TC, :], axis=AX.X,
                                            op=ALU.max).then_inc(m_full, 1)

            dve.wait_ge(cst, 7)
            for n in range(NI):
                max_item(0, n)
            with dve.Fori(0, NG - 1) as g:
                for n in range(NI):
                    max_item(g + 1, n)
            ffn.dve(dve, psS, psM, psO)
            fin.dve(dve, link, route, psS, X)

        @block.tensor
        def _(pe):
            pe.wait_ge(cst, 10)
            for k in range(NC):
                pe.wait_ge(xn_ok, k + 1)
                for i in range(TC):
                    last = nc.tensor.transpose(psS[:, k, i * P:(i + 1) * P], xn[:, k * TC + i, :], ident[:, :])
                last.then_inc(xt_ps, 1)
            pe.wait_ge(w_in, 48)
            for k in range(NC):
                pe.wait_ge(xt_ok, k + 1)
                for w in range(2):
                    n = 2 * k + w
                    if n >= 3:
                        pe.wait_ge(r1_ok, n - 2)
                    nc.tensor.matmul(psM[:, n % 3, :], wqkv_sb[:, (1 - w) * D:(2 - w) * D],
                                     xnT[:, k * CW:(k + 1) * CW], start=True, stop=True).then_inc(qk_ps, 1)
                for i in range(TC):
                    last = nc.tensor.matmul(psS[:, k, i * D:(i + 1) * D], xnT[:, k * CW + i * P:k * CW + (i + 1) * P],
                                            wqkv_sb[:, 2 * D:3 * D], start=True, stop=True)
                last.then_inc(v_ps, 1)
            for i in range(NT):
                last = nc.tensor.matmul(psO[:, i * E:(i + 1) * E], xnT[:, i * P:(i + 1) * P], gate_sb[:, :],
                                        start=True, stop=True)
            last.then_inc(lg_ps, 1)
            route.pe(pe, psO, before, ones)

            def max_item(gm, n):
                it = ITEMS[n]
                if n >= 3:
                    pe.wait_ge(m_red, gm * NI + n - 2)
                elif not (isinstance(gm, int) and gm == 0):
                    pe.wait_ge(m_red, gm * NI)
                if it[0] == "turn":
                    wait_apart(pe, m_cut, gm * NC + it[1] + 1, p_passed)
                    nc.tensor.transpose(psM[:, n % 3, :].bitcast(BF16)[0:NPART * HG * TC, 0:P],
                                        msplit[:, it[1], :, :].rearrange("p a m -> p (a m)"), identb[:, :]
                                        ).then_inc(m_mm, 1)
                    return
                _, i, c, h = it
                if i % TC == 0 and h == 0:
                    if c == 0:
                        pe.wait_ge(qb_in[i // TC], gm * (16 * 9) + 16 * 9)
                    if c == i // TC:
                        pe.wait_ge(kb_in[c], gm * 48 + 48)
                w = block_width(i, c)
                nc.tensor.matmul(psM[:, n % 3, 0:w], QB[0:SK, h, i * P:(i + 1) * P], KB[0:SK, h, c * CW:c * CW + w],
                                 start=True, stop=True).then_inc(m_mm, 1)

            def scores(g, q, p):
                c, j = UNITS[q]
                first, w = unit_columns(c, j)
                if q >= 1:
                    pe.wait_ge(s_exp, g * NPAIR + 2 * q + p - 1)
                if j == 0 and p == 0:
                    pe.wait_ge(qa_in[c], g * 160 + 160)
                if j == TC * c and p == 0:
                    pe.wait_ge(ka_in[c], g * 48 + 48)
                for u in range(2):
                    h = 2 * p + u
                    last = nc.tensor.matmul(psS[:, h, 0:w], KA[0:SKM, h, j * P:(j + 1) * P],
                                            QA[0:SKM, h, c * CW + first:(c + 1) * CW],
                                            start=True, stop=j < TC * c)
                    if j >= TC * c:
                        last = nc.tensor.matmul(psS[:, h, 0:P], identb[:, :], behind[:, :], start=False, stop=True)
                last.then_inc(s_mm, 1)

            def weigh(g, q):
                c, j = UNITS[q]
                first, w = unit_columns(c, j)
                pe.wait_ge(s_exp, g * NPAIR + 2 * q + 2)
                if j == TC * c:
                    pe.wait_ge(va_in[c], g * 16 + 16)
                if j == 0:
                    pe.wait_ge(o_row, g * NC + c + 1)
                for h in range(HG):
                    last = nc.tensor.matmul(psO[32 * h:32 * h + VW, first:CW], VA[:, j, h, :], probs[:, q % 2, h, 0:w],
                                            start=(j == 0), stop=(j == TC * c + TC - 1))
                last.then_inc(o_mm, 1)

            def attention(g, with_max):
                for q in range(NU):
                    n0, n1 = SHARE[q] if with_max else (0, 0)
                    mid = n0 + (n1 - n0) // 2
                    scores(g, q, 0)
                    for n in range(n0, mid):
                        max_item(g + 1, n)
                    if q:
                        weigh(g, q - 1)
                    scores(g, q, 1)
                    for n in range(mid, n1):
                        max_item(g + 1, n)
                weigh(g, NU - 1)

            pe.wait_ge(v_ok, NC)
            pe.wait_ge(o_zero, 1)
            for n in range(NI):
                max_item(0, n)
            with pe.Fori(0, NG - 1) as g:
                attention(g, True)
            pe.wait_ge(o_row, NC * (NG - 1) + 1)
            pe.wait_ge(m_red, NI * NG)
            pe.wait_ge(ew_in, 16 * (2 + E))
            ffn.pe(pe, ident, psS, psM, psO, W1, W3, W2, route)
            attention(NG - 1, False)
            fin.pe(pe, psS, wo_sb)


def wait_apart(eng, sem, value, passed):
    eng.wait_ge(sem, value)
    if not isinstance(value, int):
        eng.sem_inc(passed, 1)


class Route:

    def __init__(self, nc, sb, sem, zeros):
        self.nc = nc
        self.zeros = zeros
        t = lambda name, dt=F32: sb("rt_" + name, [P, NT, E], dt)
        self.L, self.L2, self.oh1, self.oh2, self.oh = t("L"), t("L2"), t("oh1"), t("oh2"), t("oh")
        self.key, self.absl, self.d1, self.d2 = t("key"), t("absl"), t("d1"), t("d2")
        self.fac, self.keep, self.e1, self.e2 = t("fac"), t("keep"), t("e1"), t("e2")
        self.desc = sb("rt_desc", [P, E])
        self.m1, self.m2, self.k1, self.k2 = (sb(f"rt_{n}", [P, NT]) for n in ("m1", "m2", "k1", "k2"))
        self.s1, self.s2, self.w1, self.w2 = (sb(f"rt_{n}", [P, NT]) for n in ("s1", "s2", "w1", "w2"))
        self.cum = [sb(f"rt_cum{b}", [P, 8 + NT, E]) for b in range(2)]
        self.pre = t("pre")
        self.tot = t("tot")
        self.slot = t("slot")
        self.over = sb("rt_over", [P, E, NT])
        self.steps = sb("rt_steps", [P, NT])
        self.tiles = [sb(f"rt_tiles{b}", [P, 4 + E]) for b in range(2)]
        self.ntile = sb("rt_ntile", [P, E])
        self.base = sb("rt_base", [P, E])
        self.sf = [sb(f"rt_sf{b}", [P, NT]) for b in range(2)]
        self.si = [sb(f"rt_si{b}", [P, NT], I32) for b in range(2)]
        self.tau = sb("rt_tau", [P, MT])
        self.tcmp = sb("rt_tcmp", [P, MT, E - 1])
        self.texp = sb("rt_texp", [P, MT])
        self.tile_expert = sb("rt_tile_expert", [P, MT], I32)
        self.zeroed = sem("rt_zeroed")
        self.filled = sem("rt_filled")
        self.cst = sem("rt_cst")
        self.d_ok = sem("rt_d_ok")
        self.e_ok = sem("rt_e_ok")
        self.oh_ok = sem("rt_oh_ok")
        self.pre_ps = sem("rt_pre_ps")
        self.slots_ok = sem("rt_slots_ok")
        self.scattered = sem("rt_scattered")

    def pool_constants(self, pool):
        nc = self.nc
        nc.gpsimd.memset(self.zeros[:, :], 0.0).then_inc(self.zeroed, 1)
        nc.gpsimd.iota(self.desc[:, :], [[-1, E]], base=E, channel_multiplier=0,
                       allow_small_or_imprecise_dtypes=True).then_inc(self.cst, 1)
        nc.gpsimd.iota(self.steps[:, :], [[P, NT]], base=0, channel_multiplier=0,
                       allow_small_or_imprecise_dtypes=True).then_inc(self.cst, 1)
        nc.gpsimd.iota(self.tau[:, :], [[1, MT]], base=0, channel_multiplier=0,
                       allow_small_or_imprecise_dtypes=True).then_inc(self.cst, 1)

    def act(self, act):
        act.wait_ge(self.d_ok, 1)
        self.nc.scalar.activation(self.e1[:, :, :], self.d1[:, :, :], ACT.Exp, scale=-1.0).then_inc(self.e_ok, 1)
        act.wait_ge(self.d_ok, 2)
        self.nc.scalar.activation(self.e2[:, :, :], self.d2[:, :, :], ACT.Exp, scale=-1.0).then_inc(self.e_ok, 1)

    def pe(self, pe, psO, before, ones):
        nc = self.nc
        pe.wait_ge(self.oh_ok, 1)
        ohf = self.oh[:, :, :].rearrange("p i e -> p (i e)")
        nc.tensor.matmul(psO[:, 128:256], before[:, :], ohf, start=True, stop=True)
        nc.tensor.matmul(psO[:, 256:384], ones[:, :], ohf, start=True, stop=True).then_inc(self.pre_ps, 1)

    def dve(self, dve, link, psO):
        nc = self.nc
        v = nc.vector
        A = lambda t: t[:, :, :]
        over_e = lambda t: t[:, :].unsqueeze(2).to_broadcast([P, NT, E])
        desc = self.desc[:, :].unsqueeze(1).to_broadcast([P, NT, E])
        dve.wait_ge(self.cst, 3)
        for t in (*self.cum, *self.tiles):
            last = v.memset(t[...] if False else (t[:, :, :] if len(t.shape) == 3 else t[:, :]), 0.0)
        link(v.tensor_copy(A(self.L), psO[:, 0:NT * E].rearrange("p (i e) -> p i e", e=E)))
        link(v.tensor_reduce(out=self.m1[:, :], in_=A(self.L), axis=AX.X, op=ALU.max))
        link(v.tensor_tensor(A(self.key), A(self.L), over_e(self.m1), ALU.is_equal))
        link(v.tensor_tensor(A(self.key), A(self.key), desc, ALU.mult))
        link(v.tensor_reduce(out=self.k1[:, :], in_=A(self.key), axis=AX.X, op=ALU.max))
        link(v.tensor_tensor(A(self.oh1), over_e(self.k1), desc, ALU.is_equal))
        link(v.scalar_tensor_tensor(out=A(self.L2), in0=A(self.oh1), scalar=NEG, in1=A(self.L),
                                    op0=ALU.mult, op1=ALU.add))
        link(v.tensor_reduce(out=self.m2[:, :], in_=A(self.L2), axis=AX.X, op=ALU.max))
        link(v.tensor_tensor(A(self.key), A(self.L2), over_e(self.m2), ALU.is_equal))
        link(v.tensor_tensor(A(self.key), A(self.key), desc, ALU.mult))
        link(v.tensor_reduce(out=self.k2[:, :], in_=A(self.key), axis=AX.X, op=ALU.max))
        link(v.tensor_tensor(A(self.oh2), over_e(self.k2), desc, ALU.is_equal))
        v.tensor_tensor(A(self.oh), A(self.oh1), A(self.oh2), ALU.add).then_inc(self.oh_ok, 1)
        v.tensor_tensor(A(self.d1), over_e(self.m1), A(self.L), ALU.subtract).then_inc(self.d_ok, 1)
        v.scalar_tensor_tensor(out=A(self.absl), in0=A(self.L), scalar=-1.0, in1=A(self.L), op0=ALU.mult, op1=ALU.max)
        link(v.tensor_tensor(A(self.key), over_e(self.m2), A(self.L), ALU.subtract))
        v.tensor_scalar(A(self.d2), A(self.key), 0.0, None, ALU.max).then_inc(self.d_ok, 1)
        link(v.tensor_tensor(A(self.fac), A(self.absl), over_e(self.m1), ALU.max))
        link(v.scalar_tensor_tensor(out=A(self.keep), in0=A(self.fac), scalar=JITTER2, in1=A(self.d1),
                                    op0=ALU.mult, op1=ALU.is_ge))
        dve.wait_ge(self.e_ok, 1)
        link(v.tensor_tensor(A(self.keep), A(self.keep), A(self.e1), ALU.mult))
        link(v.tensor_reduce(out=self.s1[:, :], in_=A(self.keep), axis=AX.X, op=ALU.add))
        v.reciprocal(self.w1[:, :], self.s1[:, :])
        link(v.tensor_tensor(A(self.fac), A(self.absl), over_e(self.m2), ALU.max))
        link(v.scalar_tensor_tensor(out=A(self.keep), in0=A(self.fac), scalar=JITTER2, in1=A(self.key),
                                    op0=ALU.mult, op1=ALU.is_ge))
        link(v.tensor_tensor(A(self.keep), A(self.keep), A(self.oh1), ALU.is_gt))
        dve.wait_ge(self.e_ok, 2)
        link(v.tensor_tensor(A(self.keep), A(self.keep), A(self.e2), ALU.mult))
        link(v.tensor_reduce(out=self.s2[:, :], in_=A(self.keep), axis=AX.X, op=ALU.add))
        link(v.reciprocal(self.w2[:, :], self.s2[:, :]))
        dve.wait_ge(self.pre_ps, 1)
        link(v.tensor_copy(A(self.pre), psO[:, 128:256].rearrange("p (i e) -> p i e", e=E)))
        link(v.tensor_copy(A(self.tot), psO[:, 256:384].rearrange("p (i e) -> p i e", e=E)))
        link(v.tensor_copy(self.cum[0][:, 8:, :], A(self.tot)))
        b = 0
        for k in (1, 2, 4, 8):
            link(v.tensor_tensor(self.cum[1 - b][:, 8:, :], self.cum[b][:, 8:, :], self.cum[b][:, 8 - k:8 + NT - k, :],
                                 ALU.add))
            b = 1 - b
        cum = self.cum[b]
        count = cum[:, 8 + NT - 1, :]
        link(v.tensor_tensor(self.over[:, :, :], count.unsqueeze(2).to_broadcast([P, E, NT]),
                             self.steps[:, :].unsqueeze(1).to_broadcast([P, E, NT]), ALU.is_gt))
        link(v.tensor_reduce(out=self.ntile[:, :], in_=self.over[:, :, :], axis=AX.X, op=ALU.add))
        link(v.tensor_copy(self.tiles[0][:, 4:], self.ntile[:, :]))
        t = 0
        for k in (1, 2, 4):
            link(v.tensor_tensor(self.tiles[1 - t][:, 4:], self.tiles[t][:, 4:], self.tiles[t][:, 4 - k:4 + E - k], ALU.add))
            t = 1 - t
        upto = self.tiles[t][:, 4:]
        link(v.tensor_tensor(self.base[:, :], upto, self.ntile[:, :], ALU.subtract))
        link(v.tensor_tensor(A(self.slot), cum[:, 8:, :], A(self.tot), ALU.subtract))
        link(v.tensor_tensor(A(self.slot), A(self.slot), A(self.pre), ALU.add))
        link(v.scalar_tensor_tensor(out=A(self.slot), in0=self.base[:, :].unsqueeze(1).to_broadcast([P, NT, E]),
                                    scalar=float(P), in1=A(self.slot), op0=ALU.mult, op1=ALU.add))
        for b, oh in enumerate((self.oh1, self.oh2)):
            link(v.tensor_tensor(A(self.key), A(self.slot), A(oh), ALU.mult))
            link(v.tensor_reduce(out=self.sf[b][:, :], in_=A(self.key), axis=AX.X, op=ALU.add))
            v.tensor_copy(self.si[b][:, :], self.sf[b][:, :]).then_inc(self.slots_ok, 1)
        link(v.tensor_tensor(self.tcmp[:, :, :], self.tau[:, :].unsqueeze(2).to_broadcast([P, MT, E - 1]),
                             upto[:, 0:E - 1].unsqueeze(1).to_broadcast([P, MT, E - 1]), ALU.is_ge))
        link(v.tensor_reduce(out=self.texp[:, :], in_=self.tcmp[:, :, :], axis=AX.X, op=ALU.add))
        v.tensor_copy(self.tile_expert[:, :], self.texp[:, :]).then_inc(self.slots_ok, 1)

    def pool_slots(self, pool):
        pool.wait_ge(self.slots_ok, 3)
        pool.wait_ge(self.filled, 48)

    def scatter(self, pool, xn, slot_x, n):
        i, b = n // 2, n % 2
        pool.indirect_dma_start(
            out=slot_x, out_offset=bass.IndirectOffsetOnAxis(ap=self.si[b][:, i:i + 1].bitcast(U32), axis=0),
            in_=xn[:, i, :], in_offset=None).then_inc(self.scattered, 16)


class Ffn:

    STEPS = MT + 3
    FIRST, BODY = 6, 6
    AHEAD = 2

    def __init__(self, nc, sb, sem, probs):
        self.nc = nc
        self.xg = sb("ff_xg", [P, 3, D])
        self.xT = sb("ff_xT", [P, 2, P])
        self.sg = probs[:, 0:2, :]
        self.hh = probs[:, 2:4, :]
        self.hT = probs[:, 4:6, :]
        self.y = sb("ff_y", [P, 3, D])
        self.x_in = [sem(f"ff_x_in{u}") for u in range(3)]
        self.y_out = [sem(f"ff_y_out{u}") for u in range(3)]
        self.t_mm = sem("ff_t_mm")
        self.t_ok = sem("ff_t_ok")
        self.u1_mm = sem("ff_u1_mm")
        self.u3_mm = sem("ff_u3_mm")
        self.g_ok = sem("ff_g_ok")
        self.h_ok = sem("ff_h_ok")
        self.ht_mm = sem("ff_ht_mm")
        self.ht_ok = sem("ff_ht_ok")
        self.y_mm = sem("ff_y_mm")
        self.y_ok = sem("ff_y_ok")

    def steps(self, eng, step):
        for s in range(self.FIRST):
            step(s, s, s // 3)
        n = (MT - self.AHEAD - self.FIRST) // self.BODY
        rest = self.FIRST + n * self.BODY
        with eng.Fori(0, n) as it:
            for v in range(self.BODY):
                step(it * self.BODY + (self.FIRST + v), self.FIRST + v, it * 2 + (self.FIRST + v) // 3)
        for s in range(rest, self.STEPS):
            step(s, s, s // 3)

    @staticmethod
    def live(s, lag):
        return not isinstance(s, int) or 0 <= s - lag < MT

    @staticmethod
    def wait(eng, sem, value):
        if not isinstance(value, int) or value > 0:
            eng.wait_ge(sem, value)

    def sp(self, sp, slot_x, slot_y, route):
        sp.wait_ge(route.scattered, 16 * 2 * NT)

        def load(s, v, k):
            if isinstance(s, int):
                if s >= MT:
                    return
                if s >= 3:
                    sp.wait_ge(self.t_mm, s - 2)
                src = slot_x[s * P:(s + 1) * P, :]
            else:
                sp.wait_ge(self.t_mm, s - 2)
                src = slot_x[bass.ds(s * P, P), :]
            sp.dma_start(self.xg[:, v % 3, :], src).then_inc(self.x_in[v % 3], 16)

        def step(s, v, k):
            load(s + self.AHEAD, v + self.AHEAD, k)
            if self.live(s, 3):
                sp.wait_ge(self.y_ok, s - 2)
                dst = slot_y[(s - 3) * P:(s - 2) * P, :] if isinstance(s, int) else slot_y[bass.ds((s - 3) * P, P), :]
                sp.dma_start(dst, self.y[:, v % 3, :]).then_inc(self.y_out[v % 3], 16)

        for s in range(self.AHEAD):
            load(s, s, 0)
        self.steps(sp, step)

    def pe(self, pe, ident, psS, psM, psO, W1, W3, W2, route):
        nc = self.nc

        def weights(tau):
            at = route.tile_expert[0:1, tau:tau + 1] if isinstance(tau, int) else route.tile_expert[0:1, bass.ds(tau, 1)]
            return pe.value_load(at, min_val=0, max_val=E - 1)

        def step(s, v, k):
            if self.live(s, 0):
                pe.wait_ge(self.x_in[v % 3], k * 16 + 16)
                self.wait(pe, self.t_ok, s)
                nc.tensor.transpose(psM[:, 2, 0:P], self.xg[:, v % 3, :], ident[:, :]).then_inc(self.t_mm, 1)
            if self.live(s, 1):
                b = (v - 1) % 2
                e = weights(s - 1)
                pe.wait_ge(self.t_ok, s)
                self.wait(pe, self.h_ok, s - 2)
                nc.tensor.matmul(psS[:, 2 * b, :], self.xT[:, b, :], W1[:, bass.ds(e * F, F)],
                                 start=True, stop=True).then_inc(self.u1_mm, 1)
                nc.tensor.matmul(psS[:, 2 * b + 1, :], self.xT[:, b, :], W3[:, bass.ds(e * F, F)],
                                 start=True, stop=True).then_inc(self.u3_mm, 1)
            if self.live(s, 2):
                b = (v - 2) % 2
                pe.wait_ge(self.h_ok, s - 1)
                self.wait(pe, self.ht_ok, s - 3)
                for c in range(FC):
                    last = nc.tensor.transpose(psM[:, b, c * P:(c + 1) * P], self.hh[:, b, c * P:(c + 1) * P],
                                               ident[:, :])
                last.then_inc(self.ht_mm, 1)
            if self.live(s, 3):
                b = (v - 3) % 2
                e = weights(s - 3)
                pe.wait_ge(self.ht_ok, s - 2)
                self.wait(pe, self.y_ok, s - 3)
                for c in range(FC):
                    last = nc.tensor.matmul(psO[:, 0:D], self.hT[:, b, c * P:(c + 1) * P],
                                            W2[:, bass.ds(e * (FC * D) + c * D, D)], start=(c == 0), stop=(c == FC - 1))
                last.then_inc(self.y_mm, 1)

        pe.wait_ge(route.slots_ok, 3)
        self.steps(pe, step)
        pe.wait_ge(self.h_ok, MT)
        pe.wait_ge(self.y_ok, MT)

    def dve(self, dve, psS, psM, psO):
        nc = self.nc

        def step(s, v, k):
            if self.live(s, 0):
                dve.wait_ge(self.t_mm, s + 1)
                self.wait(dve, self.u3_mm, s - 1)
                nc.vector.tensor_copy(self.xT[:, v % 2, :], psM[:, 2, 0:P]).then_inc(self.t_ok, 1)
            if self.live(s, 1):
                b = (v - 1) % 2
                dve.wait_ge(self.g_ok, s)
                dve.wait_ge(self.u3_mm, s)
                self.wait(dve, self.ht_mm, s - 2)
                nc.vector.tensor_tensor(self.hh[:, b, :], self.sg[:, b, :], psS[:, 2 * b + 1, :],
                                        ALU.mult).then_inc(self.h_ok, 1)
            if self.live(s, 3):
                dve.wait_ge(self.y_mm, s - 2)
                if isinstance(s, int):
                    self.wait(dve, self.y_out[v % 3], 16 * (k - 1))
                else:
                    dve.wait_ge(self.y_out[v % 3], k * 16 - 16)
                nc.vector.tensor_copy(self.y[:, v % 3, :], psO[:, 0:D]).then_inc(self.y_ok, 1)

        self.steps(dve, step)

    def act(self, act, psS, psM):
        nc = self.nc

        def step(s, v, k):
            if self.live(s, 1):
                b = (v - 1) % 2
                act.wait_ge(self.u1_mm, s)
                self.wait(act, self.h_ok, s - 2)
                nc.scalar.activation(self.sg[:, b, :], psS[:, 2 * b, :], ACT.Silu).then_inc(self.g_ok, 1)
            if self.live(s, 2):
                b = (v - 2) % 2
                act.wait_ge(self.ht_mm, s - 1)
                self.wait(act, self.y_mm, s - 3)
                nc.scalar.activation(self.hT[:, b, :], psM[:, b, :], ACT.Copy).then_inc(self.ht_ok, 1)

        self.steps(act, step)

    def pool(self, pool):
        for u in range(3):
            pool.wait_ge(self.y_out[u], 16 * (MT // 3))


class Final:

    def __init__(self, nc, sem, QB, KB, Vp):
        self.nc = nc
        halves = []
        for stack in (QB, KB):
            flat = stack[:, :, :].rearrange("p h n -> p (h n)").bitcast(F32)
            halves += [flat[:, b * T:(b + 1) * T] for b in range(2)]
        tiled = [half.rearrange("p (i d) -> p i d", d=D) for half in halves]
        self.rows = tiled[0:2]
        self.gate = tiled[2]
        self.res = tiled[3]
        flat = Vp[:, :, :, :].rearrange("p i h w -> p (i h w)")
        self.num, self.den = (flat[:, b * T:(b + 1) * T] for b in range(2))
        self.rows_in = sem("fn_rows_in")
        self.mix_ok = sem("fn_mix_ok")
        self.gate_ok = sem("fn_gate_ok")
        self.nd_in = [sem(f"fn_nd_in{c}") for c in range(NC)]
        self.attn_ok = sem("fn_attn_ok")
        self.proj_mm = sem("fn_proj_mm")
        self.res_ok = sem("fn_res_ok")
        self.out_ok = sem("fn_out_ok")
        self.c = sem("fn_chain")

    def gather(self, pool, route, slot_y, n):
        i, b = n // 2, n % 2
        pool.indirect_dma_start(
            out=self.rows[b][:, i, :], out_offset=None, in_=slot_y,
            in_offset=bass.IndirectOffsetOnAxis(ap=route.si[b][:, i:i + 1].bitcast(U32), axis=0),
        ).then_inc(self.rows_in, 16)

    def sp(self, sp, attn_raw, out):
        for c in range(NC):
            for dst, r in ((self.num, 0), (self.den, DK)):
                sp.dma_start(dst[:, c * CW:(c + 1) * CW],
                             attn_raw[:, r:r + DK, c * CW:(c + 1) * CW]).then_inc(self.nd_in[c], 16)
        for c in range(NC):
            sp.wait_ge(self.res_ok, c + 1)
            sp.dma_start(out[c * CW:(c + 1) * CW, :].rearrange("(i p) d -> p i d", p=P),
                         self.res[:, c * TC:(c + 1) * TC, :]).then_inc(self.out_ok, 16)
        sp.wait_ge(self.out_ok, 16 * NC)

    def act(self, act):
        for c in range(NC):
            act.wait_ge(self.mix_ok, c + 1)
            view = self.gate[:, c * TC:(c + 1) * TC, :]
            self.nc.scalar.activation(view, view, ACT.Silu).then_inc(self.gate_ok, 1)

    def dve(self, dve, link, route, psS, X):
        nc = self.nc
        dve.wait_ge(self.rows_in, 16 * 2 * NT)
        for c in range(NC):
            for i in range(c * TC, (c + 1) * TC):
                last = nc.vector.tensor_scalar(self.rows[0][:, i, :], self.rows[0][:, i, :], route.w1[:, i:i + 1], None,
                                               ALU.mult)
            link(last)
            for i in range(c * TC, (c + 1) * TC):
                last = nc.vector.scalar_tensor_tensor(out=self.gate[:, i, :], in0=self.rows[1][:, i, :],
                                                      scalar=route.w2[:, i:i + 1], in1=self.rows[0][:, i, :],
                                                      op0=ALU.mult, op1=ALU.add)
            last.then_inc(self.mix_ok, 1)
        for c in range(NC):
            cols = slice(c * CW, (c + 1) * CW)
            dve.wait_ge(self.nd_in[c], 32)
            link(nc.vector.reciprocal(self.den[:, cols], self.den[:, cols]))
            nc.vector.tensor_tensor(self.num[:, cols], self.num[:, cols], self.den[:, cols],
                                    ALU.mult).then_inc(self.attn_ok, 1)
        for c in range(NC):
            tiles = slice(c * TC, (c + 1) * TC)
            dve.wait_ge(self.proj_mm, c + 1)
            dve.wait_ge(self.gate_ok, c + 1)
            link(nc.vector.tensor_tensor(self.res[:, tiles, :], self.gate[:, tiles, :],
                                         psS[:, c, :].rearrange("p (i d) -> p i d", d=D), ALU.mult))
            nc.vector.tensor_tensor(self.res[:, tiles, :], self.res[:, tiles, :], X[:, tiles, :],
                                    ALU.add).then_inc(self.res_ok, 1)

    def pe(self, pe, psS, wo_sb):
        for c in range(NC):
            pe.wait_ge(self.attn_ok, c + 1)
            for i in range(TC):
                last = self.nc.tensor.matmul(psS[:, c, i * D:(i + 1) * D],
                                             self.num[:, c * CW + i * P:c * CW + (i + 1) * P], wo_sb[:, :],
                                             start=True, stop=True)
            last.then_inc(self.proj_mm, 1)


def kernel(L0_attn_x, L0_attn_w_qkv, L0_attn_w_o, L0_ffn_gate_w, L0_ffn_w1, L0_ffn_w2, L0_ffn_w3):
    import numpy as np
    import concourse.bacc as bacc
    from concourse.bass_utils import run_bass_kernel_spmd

    def flat(a, *axes):
        a = np.asarray(a)
        return np.ascontiguousarray(a.transpose(*axes) if axes else a)

    arrays = {
        "x": flat(L0_attn_x).reshape(T, D),
        "wqkvT": flat(flat(L0_attn_w_qkv).reshape(3 * D, D), 1, 0),
        "woT": flat(L0_attn_w_o, 1, 0),
        "gateT": flat(L0_ffn_gate_w, 1, 0),
        "w1T": flat(L0_ffn_w1, 0, 2, 1),
        "w3T": flat(L0_ffn_w3, 0, 2, 1),
        "w2T": flat(L0_ffn_w2, 0, 2, 1),
    }
    nc = bacc.Bacc("TRN2", target_bir_lowering=False, num_devices=1)
    args = {n: nc.dram_tensor(n, a.shape, F32, kind="ExternalInput").ap() for n, a in arrays.items()}
    args["out"] = nc.dram_tensor("out", (T, D), F32, kind="ExternalOutput").ap()
    build(nc, **args)
    r = run_bass_kernel_spmd(nc, [arrays], core_ids=[0])
    return r.results[0]["out"].reshape(1, T, D)
```

```python
from contextlib import ExitStack

import concourse.bass as bass
from concourse import mybir

F32 = mybir.dt.float32
BF16 = mybir.dt.bfloat16
U32 = mybir.dt.uint32
I32 = mybir.dt.int32
ALU = mybir.AluOpType
ACT = mybir.ActivationFunctionType
AX = mybir.AxisListType

P = 128
T = 2048
NT = T // P
D = 128
H = 16
DK = D // H
HG = 4
NG = H // HG
CW = 512
NC = T // CW
TC = CW // P
NPART = 3
SK = NPART * NPART * DK
SKM = SK + NPART
VW = 2 * DK
E = 8
F = 512
FC = F // P
MT = (2 * T + E * (P - 1)) // P
NEG = -3.0e38
EPS = 1e-5
JITTER2 = 2.0 * 0.01
SCALE = DK ** -0.5

UNITS = [(c, j) for c in range(NC) for j in range(TC * (c + 1))]
UNIT_AT = {u: q for q, u in enumerate(UNITS)}
NU = len(UNITS)
NPAIR = 2 * NU


def unit_columns(c, j):
    first = P * max(0, j - TC * c)
    return first, CW - first


def max_items():
    items, due = [], []
    for s in range(NC):
        for c in range(s + 1):
            for i in range(s * TC, (s + 1) * TC):
                for h in range(HG):
                    items.append(("block", i, c, h))
                    if due and len(items) >= due[0][0]:
                        items.append(("turn", due.pop(0)[1]))
        due.append((len(items) + 7, s))
    return items + [("turn", s) for _, s in due]


ITEMS = max_items()
NI = len(ITEMS)
TURN_AT = {it[1]: n for n, it in enumerate(ITEMS) if it[0] == "turn"}
LAST_BLOCK = {s: max(n for n, it in enumerate(ITEMS) if it[0] == "block" and it[1] // TC == s) for s in range(NC)}
LAST_OF_KEYS = {c: max(n for n, it in enumerate(ITEMS) if it[0] == "block" and it[2] == c) for c in range(NC)}


def block_width(i, c):
    return CW if c < i // TC else P * (i % TC + 1)


def item_cost(it):
    return block_width(it[1], it[2]) + 60 if it[0] == "block" else 60


def max_share():
    total_u = sum(unit_columns(*u)[1] + 60 for u in UNITS)
    total_i = sum(item_cost(it) for it in ITEMS)
    share, n, done_u, done_i = [], 0, 0, 0
    for u in UNITS:
        done_u += unit_columns(*u)[1] + 60
        n0 = n
        while n < NI and done_i < total_i * done_u / total_u / 0.98:
            done_i += item_cost(ITEMS[n])
            n += 1
        share.append((n0, n))
    return share


SHARE = max_share()
PROJECT_AT = {UNIT_AT[(c + 1, 0)] + 7: c for c in range(NC - 1)}
GATE_AT = NU - 5


def build(nc, x, wqkvT, woT, gateT, w1T, w3T, w2T, out):
    ctx = ExitStack()
    with ctx:
        def sb(name, shape, dt=F32):
            return ctx.enter_context(nc.sbuf_tensor(name, shape, dt))

        def sem(name):
            return ctx.enter_context(nc.semaphore(name))

        qparts = nc.dram_tensor("qparts", [NC, NPART, DK, H, CW], BF16, kind="Internal").ap()
        kparts = nc.dram_tensor("kparts", [NC, DK, NPART, H, CW], BF16, kind="Internal").ap()
        mparts = nc.dram_tensor("mparts", [NC, NPART, H, CW], BF16, kind="Internal").ap()
        attn_raw = nc.dram_tensor("attn_raw", [NG - 1, P, T], F32, kind="Internal").ap()
        slot_x = nc.dram_tensor("slot_x", [MT * P, D], F32, kind="Internal").ap()
        slot_y = nc.dram_tensor("slot_y", [MT * P, D], F32, kind="Internal").ap()

        psS = ctx.enter_context(nc.psum_tensor("psS", [P, 4, CW], F32))
        psM = ctx.enter_context(nc.psum_tensor("psM", [P, 3, CW], F32))
        psO = ctx.enter_context(nc.psum_tensor("psO", [P, CW], F32))

        X = sb("X", [P, NT, D])
        xn = sb("xn", [P, NT, D])
        xnT = sb("xnT", [P, T])
        wqkv_sb = sb("wqkv_sb", [P, 3 * D])
        wo_sb = sb("wo_sb", [P, D])
        gate_sb = sb("gate_sb", [P, E])
        W1 = sb("W1", [P, E * F])
        W3 = sb("W3", [P, E * F])
        W2 = sb("W2", [P, E * FC * D])
        stats = sb("stats", [P, NT, 6])
        mv = sb("mv", [P, NT, 2])
        var_eps = sb("var_eps", [P, NT])
        minus_half = sb("minus_half", [P, TC])
        rstd = sb("rstd", [P, NT])
        ident = sb("ident", [P, P])
        identb = sb("identb", [P, P], BF16)
        behind = sb("behind", [P, P], BF16)
        before = sb("before", [P, P])
        ones = sb("ones", [P, P])
        causal = sb("causal", [P, CW])
        zeros = sb("zeros", [P, D])
        Vp = sb("Vp", [P, NT, H, VW])
        rest = sb("rest", [P, 2, CW])
        QA = sb("QA", [P, NC, HG, CW], BF16)
        KA = sb("KA", [P, NC, HG, CW], BF16)
        QB = sb("QB", [P, NC, HG, CW], BF16)
        KB = sb("KB", [P, NC, HG, CW], BF16)
        VA = sb("VA", [P, NT, HG, VW])
        probs = sb("probs", [P, 2, HG, CW])
        junk = sb("junk", [P, 3, CW], BF16)
        QP = QA[:, :, 0:NPART, :]
        KP = probs[:, :, :, :].rearrange("p b h n -> p (b h n)").bitcast(BF16)[:, 0:NC * NPART * CW].rearrange(
            "p (c a n) -> p c a n", c=NC, a=NPART)
        mpart = sb("mpart", [P, HG, NT, NC])
        mfull = sb("mfull", [P, NC, HG * TC])
        mrest = sb("mrest", [P, NC, HG * TC])
        msplit = sb("msplit", [P, NC, NPART, HG * TC], BF16)
        mturn = sb("mturn", [NPART * HG * TC, NC, P], BF16)
        orow = xnT[:, :].rearrange("p (c n) -> p c n", c=NC)

        x_in = [sem(f"x_in{k}") for k in range(NC)]
        w_in = sem("w_in")
        ew_in = sem("ew_in")
        cst = sem("cst")
        dve_c = sem("dve_c")
        xn_ok = sem("xn_ok")
        var_ok = sem("var_ok")
        rstd_ok = sem("rstd_ok")
        xt_ps = sem("xt_ps")
        xt_ok = sem("xt_ok")
        lg_ps = sem("lg_ps")
        v_ps = sem("v_ps")
        v_ok = sem("v_ok")
        qk_ps = sem("qk_ps")
        p1_ok = sem("p1_ok")
        r1_ok = sem("r1_ok")
        p2_ok = sem("p2_ok")
        p3_ok = sem("p3_ok")
        parts_out = [sem(f"parts_out{k}") for k in range(NC)]
        kset = sem("kset")
        v_set = sem("v_set")
        o_zero = sem("o_zero")
        kb_in = [sem(f"kb_in{p}") for p in range(NC)]
        qb_in = [sem(f"qb_in{p}") for p in range(NC)]
        ka_in = [sem(f"ka_in{p}") for p in range(NC)]
        qa_in = [sem(f"qa_in{p}") for p in range(NC)]
        va_in = sem("va_in")
        m_mm = sem("m_mm")
        m_red = sem("m_red")
        m_full = sem("m_full")
        m_cut = sem("m_cut")
        m_chain = sem("m_chain")
        m_out = sem("m_out")
        d_passed, p_passed, l_passed = sem("d_passed"), sem("p_passed"), sem("l_passed")
        s_mm = sem("s_mm")
        s_exp = sem("s_exp")
        o_mm = sem("o_mm")
        o_row = sem("o_row")
        o_out = sem("o_out")
        route = Route(nc, sb, sem)
        ffn = Ffn(nc, sb, sem, probs[:, :, :, :].rearrange("p b h n -> p (b h) n"))
        fin = Final(nc, sem, QB, KB, Vp, orow)

        def group(g):
            return bass.ds(g * HG, HG)

        block = ctx.enter_context(nc.Block())

        @block.sync
        def _(sp):
            def load_k(dst, g, p, done):
                sp.dma_start(dst[0:SK, p, :, :].rearrange("r h n -> r (h n)"),
                             kparts[p, :, :, group(g), :].rearrange("k j h n -> (k j) (h n)").unsqueeze(0)
                             .to_broadcast([NPART, NPART * DK, HG * CW])).then_inc(done, 16)

            def load_q(dst, g, p, done):
                sp.dma_start(dst[0:SK, p, :, :].rearrange("r h n -> r (h n)"),
                             qparts[p, :, :, group(g), :].rearrange("i k h n -> (i k) (h n)").unsqueeze(1)
                             .to_broadcast([NPART * DK, NPART, HG * CW])).then_inc(done, 16)

            def load_m(g, p, done):
                sp.dma_start(QA[SK:SKM, p, :, :].rearrange("a h n -> a (h n)"),
                             mparts[p, :, group(g), :].rearrange("a h n -> a (h n)")).then_inc(done, 16)

            def store_m(g, s):
                sp.dma_start(mparts[s, :, group(g), :].rearrange("a h (i n) -> a (h i) n", n=P),
                             mturn[:, s, :]).then_inc(m_out, 16)

            def store_o(g, c):
                sp.dma_start(attn_raw[bass.ds(g, 1), :, c * CW:(c + 1) * CW].rearrange("a p n -> (a p) n"),
                             orow[:, c, :]).then_inc(o_out, 16)

            sp.sem_inc(o_out, 1)
            for k in range(NC):
                sp.dma_start(X[:, TC * k:TC * (k + 1), :],
                             x[k * CW:(k + 1) * CW, :].rearrange("(i p) d -> p i d", p=P)).then_inc(x_in[k], 16)
            for k in range(NC):
                sp.wait_ge(p3_ok, 2 * k + 1)
                for j in range(NPART):
                    sp.dma_start(kparts[k, :, j, :, :], KP[:, k, j, :]
                                 ).then_inc(parts_out[k], 16)
                sp.wait_ge(p3_ok, 2 * k + 2)
                sp.dma_start(qparts[k].rearrange("i k h n -> (k h) i n"), QP[:, k, :, :]).then_inc(parts_out[k], 16)
                sp.wait_ge(parts_out[k], 64)
                load_k(KB, 0, k, kb_in[k])
                load_q(QB, 0, k, qb_in[k])
            sp.wait_ge(kset, 1)
            for p in range(NC):
                load_k(KA, 0, p, ka_in[p])
                load_q(QA, 0, p, qa_in[p])
            sp.wait_ge(route.zeroed, 1)
            sp.dma_start(slot_x.rearrange("(i p) d -> p i d", p=P),
                         zeros[:, :].unsqueeze(1).to_broadcast([P, MT, D])).then_inc(route.filled, 16)
            for s in range(NC):
                sp.wait_ge(m_red, TURN_AT[s] + 1)
                store_m(0, s)
                sp.wait_ge(m_mm, LAST_BLOCK[s] + 1)
                load_q(QB, 1, s, qb_in[s])
                sp.wait_ge(m_out, 16 * (s + 1))
                load_m(0, s, qa_in[s])
            for p in range(NC):
                load_k(KB, 1, p, kb_in[p])

            with sp.Fori(0, NG - 1) as g:
                nxt = (g + 2) % NG
                for c in range(NC):
                    if c == NC - 1:
                        for p in range(NC - 1):
                            q = UNIT_AT[(c, TC * p + TC - 1)]
                            sp.wait_ge(s_mm, NPAIR * g + 2 * q + 2)
                            load_k(KA, g + 1, p, ka_in[p])
                            sp.wait_ge(m_mm, NI * (g + 1) + LAST_OF_KEYS[p] + 1)
                            load_k(KB, nxt, p, kb_in[p])
                    sp.wait_ge(m_red, NI * (g + 1) + TURN_AT[c] + 1)
                    store_m(g + 1, c)
                    load_q(QB, nxt, c, qb_in[c])
                    if c == NC - 1:
                        load_k(KB, nxt, c, kb_in[c])
                    q = UNIT_AT[(c, TC * c + TC - 1)]
                    sp.wait_ge(s_mm, NPAIR * g + 2 * q + 2)
                    if c == NC - 1:
                        load_k(KA, g + 1, c, ka_in[c])
                    load_q(QA, g + 1, c, qa_in[c])
                    sp.wait_ge(m_out, (16 * NC) * (g + 1) + 16 * (c + 1))
                    load_m(g + 1, c, qa_in[c])
                    sp.wait_ge(o_row, NC * g + c + 2)
                    store_o(g, c)

            ffn.sp(sp, slot_x, slot_y, route)

            sp.wait_ge(o_out, 16 * (NG - 1) * NC + 1)
            sp.wait_ge(va_in, NG * NC)
            fin.sp(sp, attn_raw, out, o_row, NC * (NG - 1) + 1)

        @block.gpsimd
        def _(pool):
            nc.gpsimd.memset(ident[:, :], 0.0).then_inc(cst, 1)
            nc.gpsimd.memset(ones[:, :], 1.0).then_inc(cst, 1)
            nc.gpsimd.memset(causal[:, :], 0.0).then_inc(cst, 1)
            nc.gpsimd.memset(zeros[:, :], 0.0).then_inc(route.zeroed, 1)
            nc.gpsimd.memset(minus_half[:, :], -0.5).then_inc(cst, 1)
            pool.wait_ge(cst, 4)
            nc.gpsimd.affine_select(out=ident[:, :], in_=ident[:, :], compare_op=ALU.not_equal, fill=1.0,
                                    base=0, pattern=[[-1, P]], channel_multiplier=1).then_inc(cst, 1)
            nc.gpsimd.affine_select(out=before[:, :], in_=ones[:, :], compare_op=ALU.is_gt, fill=0.0,
                                    base=0, pattern=[[1, P]], channel_multiplier=-1).then_inc(cst, 1)
            nc.gpsimd.affine_select(out=causal[:, CW - P:], in_=causal[:, CW - P:], compare_op=ALU.is_ge, fill=NEG,
                                    base=0, pattern=[[-1, P]], channel_multiplier=1).then_inc(cst, 1)
            pool.wait_ge(cst, 5)
            nc.gpsimd.tensor_copy(identb[:, :], ident[:, :]).then_inc(cst, 1)
            nc.gpsimd.memset(behind[:, :], 0.0).then_inc(cst, 1)
            pool.wait_ge(cst, 9)
            nc.gpsimd.affine_select(out=behind[:, :], in_=behind[:, :], compare_op=ALU.is_ge, fill=NEG,
                                    base=0, pattern=[[1, P]], channel_multiplier=-1).then_inc(cst, 1)
            for k in range(NC):
                pool.wait_ge(var_ok, k + 1)
                nc.gpsimd.tensor_tensor(rstd[:, TC * k:TC * k + TC], var_eps[:, TC * k:TC * k + TC],
                                        minus_half[:, 0:TC], ALU.pow).then_inc(rstd_ok, 1)
            route.pool_constants(pool)
            nc.gpsimd.memset(Vp[:, :, :, :], 1.0).then_inc(v_set, 1)
            pool.wait_ge(v_set, 1)
            nc.gpsimd.memset(KA[64:96, :, :, :], -1.0).then_inc(kset, 1)
            pool.wait_ge(kset, 1)
            for n in range(2 * NC):
                dst = (KP, QP)[n % 2]
                pool.wait_ge(p2_ok, n + 1)
                nc.gpsimd.tensor_tensor(dst[:, n // 2, 2, :], rest[:, n % 2, :], dst[:, n // 2, 1, :],
                                        ALU.subtract).then_inc(p3_ok, 1)

            def place_v(g, p):
                nc.gpsimd.tensor_copy(VA[:, p * TC:(p + 1) * TC, :, :],
                                      Vp[:, p * TC:(p + 1) * TC, group(g), :]).then_inc(va_in, 1)

            def cut_maxima(gm, s):
                wait_apart(pool, m_full, gm * NC + s + 1, l_passed)
                nc.gpsimd.tensor_copy(msplit[:, s, 0, :], mfull[:, s, :]).then_inc(m_chain, 1)
                pool.wait_ge(m_chain, gm * (3 * NC) + 3 * s + 1)
                nc.gpsimd.tensor_tensor(mrest[:, s, :], mfull[:, s, :], msplit[:, s, 0, :],
                                        ALU.subtract).then_inc(m_chain, 1)
                wait_apart(pool, m_chain, gm * (3 * NC) + 3 * s + 2, l_passed)
                nc.gpsimd.tensor_copy(msplit[:, s, 1, :], mrest[:, s, :]).then_inc(m_chain, 1)
                pool.wait_ge(m_chain, gm * (3 * NC) + 3 * s + 3)
                nc.gpsimd.tensor_tensor(msplit[:, s, 2, :], mrest[:, s, :], msplit[:, s, 1, :],
                                        ALU.subtract).then_inc(m_cut, 1)

            for p in range(NC):
                pool.wait_ge(v_ok, p + 1)
                place_v(0, p)
            route.pool_slots(pool)
            n = 0
            for s, upto in enumerate((4, 12, 22, 2 * NT)):
                while n < upto:
                    route.scatter(pool, xn, slot_x, n)
                    n += 1
                cut_maxima(0, s)

            with pool.Fori(0, NG - 1) as g:
                for s in range(NC - 1):
                    cut_maxima(g + 1, s)
                for p in range(NC):
                    if p == NC - 1:
                        cut_maxima(g + 1, p)
                    wait_apart(pool, o_mm, NU * g + UNIT_AT[(NC - 1, TC * p + TC - 1)] + 1, l_passed)
                    place_v(g + 1, p)
            ffn.pool(pool)
            for p in range(NC):
                pool.wait_ge(qb_in[p], 16 * (NG + 1))
                pool.wait_ge(kb_in[p], 16 * (NG + 1))
            for n in range(2 * NT):
                fin.gather(pool, route, slot_y, n)

        @block.scalar
        def _(act):
            act.sem_inc(o_row, 1)
            act.dma_start(wqkv_sb[:, :], wqkvT).then_inc(w_in, 16)
            act.dma_start(gate_sb[:, :], gateT).then_inc(w_in, 16)
            act.dma_start(wo_sb[:, :], woT).then_inc(w_in, 16)
            for k in range(NC):
                act.wait_ge(xt_ps, k + 1)
                nc.scalar.activation(xnT[:, k * CW:(k + 1) * CW], psS[:, k, :], ACT.Copy).then_inc(xt_ok, 1)
            act.wait_ge(v_set, 1)
            for n in range(2 * NC):
                dst = (KP, QP)[n % 2]
                act.wait_ge(qk_ps, n + 1)
                nc.scalar.activation(dst[:, n // 2, 0, :], psM[:, n % 3, :], ACT.Copy).then_inc(p1_ok, 1)
                act.wait_ge(r1_ok, n + 1)
                nc.scalar.activation(dst[:, n // 2, 1, :], rest[:, n % 2, :], ACT.Copy).then_inc(p2_ok, 1)
                if n % 2:
                    k = n // 2
                    act.wait_ge(v_ps, k + 1)
                    nc.scalar.activation(Vp[:, k * TC:(k + 1) * TC, :, 0:DK],
                                         psS[:, k, :].rearrange("p (j h w) -> p j h w", j=TC, h=H),
                                         ACT.Copy).then_inc(v_ok, 1)
            route.act(act)
            act.wait_ge(m_mm, 64)
            act.dma_start(W1[:, :].rearrange("p (e f) -> p e f", e=E), w1T.rearrange("e p f -> p e f")).then_inc(ew_in, 16)
            act.wait_ge(m_mm, 90)
            act.dma_start(W3[:, :].rearrange("p (e f) -> p e f", e=E), w3T.rearrange("e p f -> p e f")).then_inc(ew_in, 16)
            act.wait_ge(m_mm, 120)
            for e in range(E):
                act.dma_start(W2[:, e * FC * D:(e + 1) * FC * D].rearrange("p (c d) -> p c d", c=FC),
                              w2T[e].rearrange("(c p) d -> p c d", p=P)).then_inc(ew_in, 16)

            def evacuate(g, c):
                act.wait_ge(o_mm, g * NU + UNIT_AT[(c, TC * c + TC - 1)] + 1)
                act.wait_ge(o_out, g * (16 * NC) + 1)
                nc.scalar.activation(orow[:, c, :], psO[:, :], ACT.Copy).then_inc(o_row, 1)

            def exps(g):
                for q, (c, j) in enumerate(UNITS):
                    if isinstance(g, int) and q == GATE_AT:
                        fin.act(act)
                    first, w = unit_columns(c, j)
                    for p in range(2):
                        act.wait_ge(s_mm, g * NPAIR + 2 * q + p + 1)
                        if p == 0 and q >= 2:
                            act.wait_ge(o_mm, g * NU + q - 1)
                        nc.scalar.activation(probs[:, q % 2, 2 * p:2 * p + 2, 0:w], psS[:, 2 * p:2 * p + 2, 0:w],
                                             ACT.Exp, scale=SCALE).then_inc(s_exp, 1)
                        if p == 0 and j == 0 and c > 0:
                            evacuate(g, c - 1)
                evacuate(g, NC - 1)

            with act.Fori(0, NG - 1) as g:
                exps(g)
            ffn.act(act, psS, psM)
            exps(NG - 1)
            act.wait_ge(o_row, NC * NG + 1)
            fin.place(act, fin.num, 0, NC - 1)

        @block.vector
        def _(dve):
            chain = [0]

            def link(ins):
                chain[0] += 1
                ins.then_inc(dve_c, 1)
                dve.wait_ge(dve_c, chain[0])

            def normalise(k):
                dve.wait_ge(rstd_ok, k + 1)
                for i in range(TC * k, TC * k + TC):
                    last = nc.vector.tensor_scalar(xn[:, i, :], X[:, i, :], mv[:, i, 0:1], rstd[:, i:i + 1],
                                                   ALU.subtract, ALU.mult)
                last.then_inc(xn_ok, 1)

            nc.vector.memset(mpart[:, :, :, :], NEG)
            nc.vector.memset(psO[:, :], 0.0).then_inc(o_zero, 1)
            for k in range(NC):
                dve.wait_ge(x_in[k], 16)
                for i in range(TC * k, TC * k + TC):
                    last = nc.vector.bn_stats(stats[:, i, :], X[:, i, :])
                link(last)
                for i in range(TC * k, TC * k + TC):
                    last = nc.vector.bn_aggr(mv[:, i, :], stats[:, i, :])
                link(last)
                nc.vector.tensor_scalar(var_eps[:, TC * k:TC * k + TC], mv[:, TC * k:TC * k + TC, 1], EPS, None,
                                        ALU.add).then_inc(var_ok, 1)
                if k:
                    normalise(k - 1)
            normalise(NC - 1)
            for n in range(2 * NC):
                dst = (KP, QP)[n % 2]
                dve.wait_ge(p1_ok, n + 1)
                if n >= 2:
                    dve.wait_ge(p3_ok, n - 1)
                nc.vector.tensor_tensor(rest[:, n % 2, :], psM[:, n % 3, :], dst[:, n // 2, 0, :],
                                        ALU.subtract).then_inc(r1_ok, 1)
            dve.wait_ge(lg_ps, 1)
            route.dve(dve, link, psO)

            def max_item(gm, n):
                it = ITEMS[n]
                if ITEMS[n][0] == "block" and ITEMS[n][2] == ITEMS[n][1] // TC:
                    wait_apart(dve, m_mm, gm * NI + n + 1, d_passed)
                else:
                    dve.wait_ge(m_mm, gm * NI + n + 1)
                if it[0] == "turn":
                    if not isinstance(gm, int):
                        dve.wait_ge(m_out, gm * (16 * NC))
                    nc.vector.tensor_copy(mturn[:, it[1], :], psM[:, n % 3, :].bitcast(BF16)[0:NPART * HG * TC, 0:P]
                                          ).then_inc(m_red, 1)
                    return
                _, i, c, h = it
                w = block_width(i, c)
                if c < i // TC:
                    nc.vector.tensor_reduce(out=mpart[:, h, i, c:c + 1], in_=psM[:, n % 3, :], axis=AX.X,
                                            op=ALU.max).then_inc(m_red, 1)
                else:
                    nc.vector.tensor_tensor_reduce(
                        out=junk[:, n % 3, 0:w], in0=psM[:, n % 3, 0:w], in1=causal[:, CW - w:], scale=1.0, scalar=NEG,
                        op0=ALU.add, op1=ALU.max, accum_out=mpart[:, h, i, c:c + 1]).then_inc(m_red, 1)
                if n in LAST_BLOCK.values():
                    s = i // TC
                    dve.wait_ge(m_red, gm * NI + n + 1)
                    nc.vector.tensor_reduce(out=mfull[:, s, :].rearrange("p (h i) -> p h i", h=HG),
                                            in_=mpart[:, :, s * TC:(s + 1) * TC, :], axis=AX.X,
                                            op=ALU.max).then_inc(m_full, 1)

            dve.wait_ge(cst, 7)
            for n in range(NI):
                max_item(0, n)
            with dve.Fori(0, NG - 1) as g:
                for n in range(NI):
                    max_item(g + 1, n)
            ffn.dve(dve, psS, psM, psO)
            fin.dve(dve, link, route, psM, X)

        @block.tensor
        def _(pe):
            pe.wait_ge(cst, 10)
            for k in range(NC):
                pe.wait_ge(xn_ok, k + 1)
                for i in range(TC):
                    last = nc.tensor.transpose(psS[:, k, i * P:(i + 1) * P], xn[:, k * TC + i, :], ident[:, :])
                last.then_inc(xt_ps, 1)
            pe.wait_ge(w_in, 48)
            for k in range(NC):
                pe.wait_ge(xt_ok, k + 1)
                for w in range(2):
                    n = 2 * k + w
                    if n >= 3:
                        pe.wait_ge(r1_ok, n - 2)
                    nc.tensor.matmul(psM[:, n % 3, :], wqkv_sb[:, (1 - w) * D:(2 - w) * D],
                                     xnT[:, k * CW:(k + 1) * CW], start=True, stop=True).then_inc(qk_ps, 1)
                for i in range(TC):
                    last = nc.tensor.matmul(psS[:, k, i * D:(i + 1) * D], xnT[:, k * CW + i * P:k * CW + (i + 1) * P],
                                            wqkv_sb[:, 2 * D:3 * D], start=True, stop=True)
                last.then_inc(v_ps, 1)
            for i in range(NT):
                last = nc.tensor.matmul(psO[:, i * E:(i + 1) * E], xnT[:, i * P:(i + 1) * P], gate_sb[:, :],
                                        start=True, stop=True)
            last.then_inc(lg_ps, 1)
            route.pe(pe, psO, before, ones)

            def max_item(gm, n):
                it = ITEMS[n]
                if n >= 3:
                    pe.wait_ge(m_red, gm * NI + n - 2)
                elif not (isinstance(gm, int) and gm == 0):
                    pe.wait_ge(m_red, gm * NI)
                if it[0] == "turn":
                    wait_apart(pe, m_cut, gm * NC + it[1] + 1, p_passed)
                    nc.tensor.transpose(psM[:, n % 3, :].bitcast(BF16)[0:NPART * HG * TC, 0:P],
                                        msplit[:, it[1], :, :].rearrange("p a m -> p (a m)"), identb[:, :]
                                        ).then_inc(m_mm, 1)
                    return
                _, i, c, h = it
                if i % TC == 0 and h == 0:
                    if c == 0:
                        pe.wait_ge(qb_in[i // TC], gm * 16 + 16)
                    if c == i // TC:
                        pe.wait_ge(kb_in[c], gm * 16 + 16)
                w = block_width(i, c)
                nc.tensor.matmul(psM[:, n % 3, 0:w], QB[0:SK, i // TC, h, i % TC * P:(i % TC + 1) * P],
                                 KB[0:SK, c, h, 0:w], start=True, stop=True).then_inc(m_mm, 1)

            def scores(g, q, p):
                c, j = UNITS[q]
                first, w = unit_columns(c, j)
                if q >= 1:
                    pe.wait_ge(s_exp, g * NPAIR + 2 * q + p - 1)
                if j == 0 and p == 0:
                    pe.wait_ge(qa_in[c], g * 32 + 32)
                if j == TC * c and p == 0:
                    pe.wait_ge(ka_in[c], g * 16 + 16)
                for u in range(2):
                    h = 2 * p + u
                    last = nc.tensor.matmul(psS[:, h, 0:w], KA[0:SKM, j // TC, h, j % TC * P:(j % TC + 1) * P],
                                            QA[0:SKM, c, h, first:CW],
                                            start=True, stop=j < TC * c)
                    if j >= TC * c:
                        last = nc.tensor.matmul(psS[:, h, 0:P], identb[:, :], behind[:, :], start=False, stop=True)
                last.then_inc(s_mm, 1)

            def weigh(g, q):
                c, j = UNITS[q]
                first, w = unit_columns(c, j)
                pe.wait_ge(s_exp, g * NPAIR + 2 * q + 2)
                if j == TC * c:
                    pe.wait_ge(va_in, g * NC + c + 1)
                if j == 0:
                    pe.wait_ge(o_row, g * NC + c + 1)
                for h in range(HG):
                    last = nc.tensor.matmul(psO[32 * h:32 * h + VW, first:CW], VA[:, j, h, :], probs[:, q % 2, h, 0:w],
                                            start=(j == 0), stop=(j == TC * c + TC - 1))
                last.then_inc(o_mm, 1)

            def attention(g, with_max):
                for q in range(NU):
                    if not with_max and q in PROJECT_AT:
                        fin.project(pe, PROJECT_AT[q], psM, wo_sb)
                    n0, n1 = SHARE[q] if with_max else (0, 0)
                    cuts = [n0 + (n1 - n0) * k // 3 for k in range(4)]
                    scores(g, q, 0)
                    for n in range(cuts[0], cuts[1]):
                        max_item(g + 1, n)
                    scores(g, q, 1)
                    for n in range(cuts[1], cuts[2]):
                        max_item(g + 1, n)
                    if q:
                        weigh(g, q - 1)
                    for n in range(cuts[2], cuts[3]):
                        max_item(g + 1, n)
                weigh(g, NU - 1)

            pe.wait_ge(v_ok, NC)
            pe.wait_ge(o_zero, 1)
            for n in range(NI):
                max_item(0, n)
            with pe.Fori(0, NG - 1) as g:
                attention(g, True)
            pe.wait_ge(o_row, NC * (NG - 1) + 1)
            pe.wait_ge(m_red, NI * NG)
            pe.wait_ge(ew_in, 16 * (2 + E))
            ffn.pe(pe, ident, psS, psM, psO, W1, W3, W2, route)
            attention(NG - 1, False)
            fin.project(pe, NC - 1, psM, wo_sb)


def wait_apart(eng, sem, value, passed):
    eng.wait_ge(sem, value)
    if not isinstance(value, int):
        eng.sem_inc(passed, 1)


class Route:

    def __init__(self, nc, sb, sem):
        self.nc = nc
        t = lambda name, dt=F32: sb("rt_" + name, [P, NT, E], dt)
        self.L, self.L2, self.oh1, self.oh2, self.oh = t("L"), t("L2"), t("oh1"), t("oh2"), t("oh")
        self.key, self.absl, self.d1, self.d2 = t("key"), t("absl"), t("d1"), t("d2")
        self.fac, self.keep, self.e1, self.e2 = t("fac"), t("keep"), t("e1"), t("e2")
        self.desc = sb("rt_desc", [P, E])
        self.m1, self.m2, self.k1, self.k2 = (sb(f"rt_{n}", [P, NT]) for n in ("m1", "m2", "k1", "k2"))
        self.s1, self.s2, self.w1, self.w2 = (sb(f"rt_{n}", [P, NT]) for n in ("s1", "s2", "w1", "w2"))
        self.cum = [sb(f"rt_cum{b}", [P, 8 + NT, E]) for b in range(2)]
        self.pre = t("pre")
        self.tot = t("tot")
        self.slot = t("slot")
        self.over = sb("rt_over", [P, E, NT])
        self.steps = sb("rt_steps", [P, NT])
        self.tiles = [sb(f"rt_tiles{b}", [P, 4 + E]) for b in range(2)]
        self.ntile = sb("rt_ntile", [P, E])
        self.base = sb("rt_base", [P, E])
        self.sf = [sb(f"rt_sf{b}", [P, NT]) for b in range(2)]
        self.si = [sb(f"rt_si{b}", [P, NT], I32) for b in range(2)]
        self.tau = sb("rt_tau", [P, MT])
        self.tcmp = sb("rt_tcmp", [P, MT, E - 1])
        self.texp = sb("rt_texp", [P, MT])
        self.tile_expert = sb("rt_tile_expert", [P, MT], I32)
        self.zeroed = sem("rt_zeroed")
        self.filled = sem("rt_filled")
        self.cst = sem("rt_cst")
        self.d_ok = sem("rt_d_ok")
        self.e_ok = sem("rt_e_ok")
        self.oh_ok = sem("rt_oh_ok")
        self.pre_ps = sem("rt_pre_ps")
        self.slots_ok = sem("rt_slots_ok")
        self.scattered = sem("rt_scattered")

    def pool_constants(self, pool):
        nc = self.nc
        nc.gpsimd.iota(self.desc[:, :], [[-1, E]], base=E, channel_multiplier=0,
                       allow_small_or_imprecise_dtypes=True).then_inc(self.cst, 1)
        nc.gpsimd.iota(self.steps[:, :], [[P, NT]], base=0, channel_multiplier=0,
                       allow_small_or_imprecise_dtypes=True).then_inc(self.cst, 1)
        nc.gpsimd.iota(self.tau[:, :], [[1, MT]], base=0, channel_multiplier=0,
                       allow_small_or_imprecise_dtypes=True).then_inc(self.cst, 1)

    def act(self, act):
        act.wait_ge(self.d_ok, 1)
        self.nc.scalar.activation(self.e1[:, :, :], self.d1[:, :, :], ACT.Exp, scale=-1.0).then_inc(self.e_ok, 1)
        act.wait_ge(self.d_ok, 2)
        self.nc.scalar.activation(self.e2[:, :, :], self.d2[:, :, :], ACT.Exp, scale=-1.0).then_inc(self.e_ok, 1)

    def pe(self, pe, psO, before, ones):
        nc = self.nc
        pe.wait_ge(self.oh_ok, 1)
        ohf = self.oh[:, :, :].rearrange("p i e -> p (i e)")
        nc.tensor.matmul(psO[:, 128:256], before[:, :], ohf, start=True, stop=True)
        nc.tensor.matmul(psO[:, 256:384], ones[:, :], ohf, start=True, stop=True).then_inc(self.pre_ps, 1)

    def dve(self, dve, link, psO):
        nc = self.nc
        v = nc.vector
        A = lambda t: t[:, :, :]
        over_e = lambda t: t[:, :].unsqueeze(2).to_broadcast([P, NT, E])
        desc = self.desc[:, :].unsqueeze(1).to_broadcast([P, NT, E])
        dve.wait_ge(self.cst, 3)
        for t in (*self.cum, *self.tiles):
            last = v.memset(t[...] if False else (t[:, :, :] if len(t.shape) == 3 else t[:, :]), 0.0)
        link(v.tensor_copy(A(self.L), psO[:, 0:NT * E].rearrange("p (i e) -> p i e", e=E)))
        link(v.tensor_reduce(out=self.m1[:, :], in_=A(self.L), axis=AX.X, op=ALU.max))
        link(v.tensor_tensor(A(self.key), A(self.L), over_e(self.m1), ALU.is_equal))
        link(v.tensor_tensor(A(self.key), A(self.key), desc, ALU.mult))
        link(v.tensor_reduce(out=self.k1[:, :], in_=A(self.key), axis=AX.X, op=ALU.max))
        link(v.tensor_tensor(A(self.oh1), over_e(self.k1), desc, ALU.is_equal))
        link(v.scalar_tensor_tensor(out=A(self.L2), in0=A(self.oh1), scalar=NEG, in1=A(self.L),
                                    op0=ALU.mult, op1=ALU.add))
        link(v.tensor_reduce(out=self.m2[:, :], in_=A(self.L2), axis=AX.X, op=ALU.max))
        link(v.tensor_tensor(A(self.key), A(self.L2), over_e(self.m2), ALU.is_equal))
        link(v.tensor_tensor(A(self.key), A(self.key), desc, ALU.mult))
        link(v.tensor_reduce(out=self.k2[:, :], in_=A(self.key), axis=AX.X, op=ALU.max))
        link(v.tensor_tensor(A(self.oh2), over_e(self.k2), desc, ALU.is_equal))
        v.tensor_tensor(A(self.oh), A(self.oh1), A(self.oh2), ALU.add).then_inc(self.oh_ok, 1)
        v.tensor_tensor(A(self.d1), over_e(self.m1), A(self.L), ALU.subtract).then_inc(self.d_ok, 1)
        v.scalar_tensor_tensor(out=A(self.absl), in0=A(self.L), scalar=-1.0, in1=A(self.L), op0=ALU.mult, op1=ALU.max)
        link(v.tensor_tensor(A(self.key), over_e(self.m2), A(self.L), ALU.subtract))
        v.tensor_scalar(A(self.d2), A(self.key), 0.0, None, ALU.max).then_inc(self.d_ok, 1)
        link(v.tensor_tensor(A(self.fac), A(self.absl), over_e(self.m1), ALU.max))
        link(v.scalar_tensor_tensor(out=A(self.keep), in0=A(self.fac), scalar=JITTER2, in1=A(self.d1),
                                    op0=ALU.mult, op1=ALU.is_ge))
        dve.wait_ge(self.e_ok, 1)
        link(v.tensor_tensor(A(self.keep), A(self.keep), A(self.e1), ALU.mult))
        link(v.tensor_reduce(out=self.s1[:, :], in_=A(self.keep), axis=AX.X, op=ALU.add))
        v.reciprocal(self.w1[:, :], self.s1[:, :])
        link(v.tensor_tensor(A(self.fac), A(self.absl), over_e(self.m2), ALU.max))
        link(v.scalar_tensor_tensor(out=A(self.keep), in0=A(self.fac), scalar=JITTER2, in1=A(self.key),
                                    op0=ALU.mult, op1=ALU.is_ge))
        link(v.tensor_tensor(A(self.keep), A(self.keep), A(self.oh1), ALU.is_gt))
        dve.wait_ge(self.e_ok, 2)
        link(v.tensor_tensor(A(self.keep), A(self.keep), A(self.e2), ALU.mult))
        link(v.tensor_reduce(out=self.s2[:, :], in_=A(self.keep), axis=AX.X, op=ALU.add))
        link(v.reciprocal(self.w2[:, :], self.s2[:, :]))
        dve.wait_ge(self.pre_ps, 1)
        link(v.tensor_copy(A(self.pre), psO[:, 128:256].rearrange("p (i e) -> p i e", e=E)))
        link(v.tensor_copy(A(self.tot), psO[:, 256:384].rearrange("p (i e) -> p i e", e=E)))
        link(v.tensor_copy(self.cum[0][:, 8:, :], A(self.tot)))
        b = 0
        for k in (1, 2, 4, 8):
            link(v.tensor_tensor(self.cum[1 - b][:, 8:, :], self.cum[b][:, 8:, :], self.cum[b][:, 8 - k:8 + NT - k, :],
                                 ALU.add))
            b = 1 - b
        cum = self.cum[b]
        count = cum[:, 8 + NT - 1, :]
        link(v.tensor_tensor(self.over[:, :, :], count.unsqueeze(2).to_broadcast([P, E, NT]),
                             self.steps[:, :].unsqueeze(1).to_broadcast([P, E, NT]), ALU.is_gt))
        link(v.tensor_reduce(out=self.ntile[:, :], in_=self.over[:, :, :], axis=AX.X, op=ALU.add))
        link(v.tensor_copy(self.tiles[0][:, 4:], self.ntile[:, :]))
        t = 0
        for k in (1, 2, 4):
            link(v.tensor_tensor(self.tiles[1 - t][:, 4:], self.tiles[t][:, 4:], self.tiles[t][:, 4 - k:4 + E - k], ALU.add))
            t = 1 - t
        upto = self.tiles[t][:, 4:]
        link(v.tensor_tensor(self.base[:, :], upto, self.ntile[:, :], ALU.subtract))
        link(v.tensor_tensor(A(self.slot), cum[:, 8:, :], A(self.tot), ALU.subtract))
        link(v.tensor_tensor(A(self.slot), A(self.slot), A(self.pre), ALU.add))
        link(v.scalar_tensor_tensor(out=A(self.slot), in0=self.base[:, :].unsqueeze(1).to_broadcast([P, NT, E]),
                                    scalar=float(P), in1=A(self.slot), op0=ALU.mult, op1=ALU.add))
        for b, oh in enumerate((self.oh1, self.oh2)):
            link(v.tensor_tensor(A(self.key), A(self.slot), A(oh), ALU.mult))
            link(v.tensor_reduce(out=self.sf[b][:, :], in_=A(self.key), axis=AX.X, op=ALU.add))
            v.tensor_copy(self.si[b][:, :], self.sf[b][:, :]).then_inc(self.slots_ok, 1)
        link(v.tensor_tensor(self.tcmp[:, :, :], self.tau[:, :].unsqueeze(2).to_broadcast([P, MT, E - 1]),
                             upto[:, 0:E - 1].unsqueeze(1).to_broadcast([P, MT, E - 1]), ALU.is_ge))
        link(v.tensor_reduce(out=self.texp[:, :], in_=self.tcmp[:, :, :], axis=AX.X, op=ALU.add))
        v.tensor_copy(self.tile_expert[:, :], self.texp[:, :]).then_inc(self.slots_ok, 1)

    def pool_slots(self, pool):
        pool.wait_ge(self.slots_ok, 3)
        pool.wait_ge(self.filled, 16)

    def scatter(self, pool, xn, slot_x, n):
        i, b = n // 2, n % 2
        pool.indirect_dma_start(
            out=slot_x, out_offset=bass.IndirectOffsetOnAxis(ap=self.si[b][:, i:i + 1].bitcast(U32), axis=0),
            in_=xn[:, i, :], in_offset=None).then_inc(self.scattered, 16)


class Ffn:

    STEPS = MT + 3
    FIRST, BODY = 6, 6
    AHEAD = 2

    def __init__(self, nc, sb, sem, probs):
        self.nc = nc
        self.xg = sb("ff_xg", [P, 3, D])
        self.xT = sb("ff_xT", [P, 2, P])
        self.sg = probs[:, 0:2, :]
        self.hh = probs[:, 2:4, :]
        self.hT = probs[:, 4:6, :]
        self.y = sb("ff_y", [P, 3, D])
        self.x_in = [sem(f"ff_x_in{u}") for u in range(3)]
        self.y_out = [sem(f"ff_y_out{u}") for u in range(3)]
        self.t_mm = sem("ff_t_mm")
        self.t_ok = sem("ff_t_ok")
        self.u1_mm = sem("ff_u1_mm")
        self.u3_mm = sem("ff_u3_mm")
        self.g_ok = sem("ff_g_ok")
        self.h_ok = sem("ff_h_ok")
        self.ht_mm = sem("ff_ht_mm")
        self.ht_ok = sem("ff_ht_ok")
        self.y_mm = sem("ff_y_mm")
        self.y_ok = sem("ff_y_ok")

    def steps(self, eng, step):
        for s in range(self.FIRST):
            step(s, s, s // 3)
        n = (MT - self.AHEAD - self.FIRST) // self.BODY
        rest = self.FIRST + n * self.BODY
        with eng.Fori(0, n) as it:
            for v in range(self.BODY):
                step(it * self.BODY + (self.FIRST + v), self.FIRST + v, it * 2 + (self.FIRST + v) // 3)
        for s in range(rest, self.STEPS):
            step(s, s, s // 3)

    @staticmethod
    def live(s, lag):
        return not isinstance(s, int) or 0 <= s - lag < MT

    @staticmethod
    def wait(eng, sem, value):
        if not isinstance(value, int) or value > 0:
            eng.wait_ge(sem, value)

    def sp(self, sp, slot_x, slot_y, route):
        sp.wait_ge(route.scattered, 16 * 2 * NT)

        def load(s, v, k):
            if isinstance(s, int):
                if s >= MT:
                    return
                if s >= 3:
                    sp.wait_ge(self.t_mm, s - 2)
                src = slot_x[s * P:(s + 1) * P, :]
            else:
                sp.wait_ge(self.t_mm, s - 2)
                src = slot_x[bass.ds(s * P, P), :]
            sp.dma_start(self.xg[:, v % 3, :], src).then_inc(self.x_in[v % 3], 16)

        def step(s, v, k):
            load(s + self.AHEAD, v + self.AHEAD, k)
            if self.live(s, 3):
                sp.wait_ge(self.y_ok, s - 2)
                dst = slot_y[(s - 3) * P:(s - 2) * P, :] if isinstance(s, int) else slot_y[bass.ds((s - 3) * P, P), :]
                sp.dma_start(dst, self.y[:, v % 3, :]).then_inc(self.y_out[v % 3], 16)

        for s in range(self.AHEAD):
            load(s, s, 0)
        self.steps(sp, step)

    def pe(self, pe, ident, psS, psM, psO, W1, W3, W2, route):
        nc = self.nc

        def weights(tau):
            at = route.tile_expert[0:1, tau:tau + 1] if isinstance(tau, int) else route.tile_expert[0:1, bass.ds(tau, 1)]
            return pe.value_load(at, min_val=0, max_val=E - 1)

        def step(s, v, k):
            if self.live(s, 0):
                pe.wait_ge(self.x_in[v % 3], k * 16 + 16)
                self.wait(pe, self.t_ok, s)
                nc.tensor.transpose(psM[:, 2, 0:P], self.xg[:, v % 3, :], ident[:, :]).then_inc(self.t_mm, 1)
            if self.live(s, 1):
                b = (v - 1) % 2
                e = weights(s - 1)
                pe.wait_ge(self.t_ok, s)
                self.wait(pe, self.h_ok, s - 2)
                nc.tensor.matmul(psS[:, 2 * b, :], self.xT[:, b, :], W1[:, bass.ds(e * F, F)],
                                 start=True, stop=True).then_inc(self.u1_mm, 1)
                nc.tensor.matmul(psS[:, 2 * b + 1, :], self.xT[:, b, :], W3[:, bass.ds(e * F, F)],
                                 start=True, stop=True).then_inc(self.u3_mm, 1)
            if self.live(s, 2):
                b = (v - 2) % 2
                pe.wait_ge(self.h_ok, s - 1)
                self.wait(pe, self.ht_ok, s - 3)
                for c in range(FC):
                    last = nc.tensor.transpose(psM[:, b, c * P:(c + 1) * P], self.hh[:, b, c * P:(c + 1) * P],
                                               ident[:, :])
                last.then_inc(self.ht_mm, 1)
            if self.live(s, 3):
                b = (v - 3) % 2
                e = weights(s - 3)
                pe.wait_ge(self.ht_ok, s - 2)
                self.wait(pe, self.y_ok, s - 3)
                for c in range(FC):
                    last = nc.tensor.matmul(psO[:, 0:D], self.hT[:, b, c * P:(c + 1) * P],
                                            W2[:, bass.ds(e * (FC * D) + c * D, D)], start=(c == 0), stop=(c == FC - 1))
                last.then_inc(self.y_mm, 1)

        pe.wait_ge(route.slots_ok, 3)
        self.steps(pe, step)
        pe.wait_ge(self.h_ok, MT)
        pe.wait_ge(self.y_ok, MT)

    def dve(self, dve, psS, psM, psO):
        nc = self.nc

        def step(s, v, k):
            if self.live(s, 0):
                dve.wait_ge(self.t_mm, s + 1)
                self.wait(dve, self.u3_mm, s - 1)
                nc.vector.tensor_copy(self.xT[:, v % 2, :], psM[:, 2, 0:P]).then_inc(self.t_ok, 1)
            if self.live(s, 1):
                b = (v - 1) % 2
                dve.wait_ge(self.g_ok, s)
                dve.wait_ge(self.u3_mm, s)
                self.wait(dve, self.ht_mm, s - 2)
                nc.vector.tensor_tensor(self.hh[:, b, :], self.sg[:, b, :], psS[:, 2 * b + 1, :],
                                        ALU.mult).then_inc(self.h_ok, 1)
            if self.live(s, 3):
                dve.wait_ge(self.y_mm, s - 2)
                if isinstance(s, int):
                    self.wait(dve, self.y_out[v % 3], 16 * (k - 1))
                else:
                    dve.wait_ge(self.y_out[v % 3], k * 16 - 16)
                nc.vector.tensor_copy(self.y[:, v % 3, :], psO[:, 0:D]).then_inc(self.y_ok, 1)

        self.steps(dve, step)

    def act(self, act, psS, psM):
        nc = self.nc

        def step(s, v, k):
            if self.live(s, 1):
                b = (v - 1) % 2
                act.wait_ge(self.u1_mm, s)
                self.wait(act, self.h_ok, s - 2)
                nc.scalar.activation(self.sg[:, b, :], psS[:, 2 * b, :], ACT.Silu).then_inc(self.g_ok, 1)
            if self.live(s, 2):
                b = (v - 2) % 2
                act.wait_ge(self.ht_mm, s - 1)
                self.wait(act, self.y_mm, s - 3)
                nc.scalar.activation(self.hT[:, b, :], psM[:, b, :], ACT.Copy).then_inc(self.ht_ok, 1)

        self.steps(act, step)

    def pool(self, pool):
        for u in range(3):
            pool.wait_ge(self.y_out[u], 16 * (MT // 3))


class Final:

    FIRST = (NG - 1) * HG * DK

    def __init__(self, nc, sem, QB, KB, Vp, orow):
        self.nc = nc
        halves = []
        for stack in (QB, KB):
            flat = stack[:, :, :, :].rearrange("p c h n -> p (c h n)").bitcast(F32)
            halves += [flat[:, b * T:(b + 1) * T] for b in range(2)]
        tiled = [half.rearrange("p (i d) -> p i d", d=D) for half in halves]
        self.rows = tiled[0:2]
        self.gate = tiled[2]
        self.res = tiled[3]
        self.orow = orow
        flat = Vp[:, :, :, :].rearrange("p i h w -> p (i h w)")
        self.num, self.den = (flat[:, b * T:(b + 1) * T] for b in range(2))
        self.rows_in = sem("fn_rows_in")
        self.mix_ok = sem("fn_mix_ok")
        self.gate_ok = sem("fn_gate_ok")
        self.nd_in = sem("fn_nd_in")
        self.nd_last = [sem(f"fn_nd_last{c}") for c in range(NC)]
        self.attn_ok = sem("fn_attn_ok")
        self.proj_mm = sem("fn_proj_mm")
        self.res_ok = sem("fn_res_ok")
        self.out_ok = sem("fn_out_ok")

    def gather(self, pool, route, slot_y, n):
        i, b = n // 2, n % 2
        pool.indirect_dma_start(
            out=self.rows[b][:, i, :], out_offset=None, in_=slot_y,
            in_offset=bass.IndirectOffsetOnAxis(ap=route.si[b][:, i:i + 1].bitcast(U32), axis=0),
        ).then_inc(self.rows_in, 16)

    def place(self, eng, dst, r, c):
        for h in range(HG):
            eng.dma_start(dst[self.FIRST + h * DK:self.FIRST + (h + 1) * DK, c * CW:(c + 1) * CW],
                          self.orow[32 * h + r:32 * h + r + DK, c, :]).then_inc(self.nd_last[c], 16)

    def sp(self, sp, attn_raw, out, o_row, rows_before):
        first = self.FIRST
        for dst, r in ((self.num, 0), (self.den, DK)):
            sp.dma_start(dst[0:first, :],
                         attn_raw.rearrange("g (h r) n -> (g h) r n", r=32)[:, r:r + DK, :]).then_inc(self.nd_in, 16)
        for c in range(NC):
            sp.wait_ge(o_row, rows_before + c + 1)
            self.place(sp, self.den, DK, c)
            if c < NC - 1:
                self.place(sp, self.num, 0, c)
        for c in range(NC):
            sp.wait_ge(self.res_ok, c + 1)
            sp.dma_start(out[c * CW:(c + 1) * CW, :].rearrange("(i p) d -> p i d", p=P),
                         self.res[:, c * TC:(c + 1) * TC, :]).then_inc(self.out_ok, 16)
        sp.wait_ge(self.out_ok, 16 * NC)

    def act(self, act):
        act.wait_ge(self.mix_ok, 1)
        self.nc.scalar.activation(self.gate, self.gate, ACT.Silu).then_inc(self.gate_ok, 1)

    def dve(self, dve, link, route, psM, X):
        nc = self.nc

        def normalise(c):
            cols = slice(c * CW, (c + 1) * CW)
            dve.wait_ge(self.nd_last[c], 16 * 2 * HG)
            link(nc.vector.reciprocal(self.den[:, cols], self.den[:, cols]))
            nc.vector.tensor_tensor(self.num[:, cols], self.num[:, cols], self.den[:, cols],
                                    ALU.mult).then_inc(self.attn_ok, 1)

        def mix():
            dve.wait_ge(self.rows_in, 16 * 2 * NT)
            for i in range(NT):
                last = nc.vector.tensor_scalar(self.rows[0][:, i, :], self.rows[0][:, i, :], route.w1[:, i:i + 1], None,
                                               ALU.mult)
            link(last)
            for i in range(NT):
                last = nc.vector.scalar_tensor_tensor(out=self.gate[:, i, :], in0=self.rows[1][:, i, :],
                                                      scalar=route.w2[:, i:i + 1], in1=self.rows[0][:, i, :],
                                                      op0=ALU.mult, op1=ALU.add)
            last.then_inc(self.mix_ok, 1)

        def residual(c):
            tiles = slice(c * TC, (c + 1) * TC)
            dve.wait_ge(self.proj_mm, c + 1)
            if c == 0:
                dve.wait_ge(self.gate_ok, 1)
            link(nc.vector.tensor_tensor(self.res[:, tiles, :], self.gate[:, tiles, :],
                                         psM[:, c % 3, :].rearrange("p (i d) -> p i d", d=D), ALU.mult))
            nc.vector.tensor_tensor(self.res[:, tiles, :], self.res[:, tiles, :], X[:, tiles, :],
                                    ALU.add).then_inc(self.res_ok, 1)

        dve.wait_ge(self.nd_in, 32)
        for c in range(NC - 1):
            normalise(c)
        mix()
        for c in range(NC - 1):
            residual(c)
        normalise(NC - 1)
        residual(NC - 1)

    def project(self, pe, c, psM, wo_sb):
        pe.wait_ge(self.attn_ok, c + 1)
        if c >= 3:
            pe.wait_ge(self.res_ok, c - 2)
        for i in range(TC):
            last = self.nc.tensor.matmul(psM[:, c % 3, i * D:(i + 1) * D],
                                         self.num[:, c * CW + i * P:c * CW + (i + 1) * P], wo_sb[:, :],
                                         start=True, stop=True)
        last.then_inc(self.proj_mm, 1)


def kernel(L0_attn_x, L0_attn_w_qkv, L0_attn_w_o, L0_ffn_gate_w, L0_ffn_w1, L0_ffn_w2, L0_ffn_w3):
    import numpy as np
    import concourse.bacc as bacc
    from concourse.bass_utils import run_bass_kernel_spmd

    def flat(a, *axes):
        a = np.asarray(a)
        return np.ascontiguousarray(a.transpose(*axes) if axes else a)

    w = flat(L0_attn_w_qkv)
    w_rows = np.concatenate([w[0:2].transpose(0, 2, 1, 3).reshape(2 * D, D), w[2].reshape(D, D)])
    arrays = {
        "x": flat(L0_attn_x).reshape(T, D),
        "wqkvT": flat(w_rows, 1, 0),
        "woT": flat(L0_attn_w_o, 1, 0),
        "gateT": flat(L0_ffn_gate_w, 1, 0),
        "w1T": flat(L0_ffn_w1, 0, 2, 1),
        "w3T": flat(L0_ffn_w3, 0, 2, 1),
        "w2T": flat(L0_ffn_w2, 0, 2, 1),
    }
    nc = bacc.Bacc("TRN2", target_bir_lowering=False, num_devices=1)
    args = {n: nc.dram_tensor(n, a.shape, F32, kind="ExternalInput").ap() for n, a in arrays.items()}
    args["out"] = nc.dram_tensor("out", (T, D), F32, kind="ExternalOutput").ap()
    build(nc, **args)
    r = run_bass_kernel_spmd(nc, [arrays], core_ids=[0])
    return r.results[0]["out"].reshape(1, T, D)
```

```python
from contextlib import ExitStack

import concourse.bass as bass
from concourse import mybir

F32 = mybir.dt.float32
BF16 = mybir.dt.bfloat16
F32R = mybir.dt.float32r
U32 = mybir.dt.uint32
I32 = mybir.dt.int32
ALU = mybir.AluOpType
ACT = mybir.ActivationFunctionType
AX = mybir.AxisListType

P = 128
T = 2048
NT = T // P
D = 128
H = 16
DK = D // H
HG = 4
NG = H // HG
CW = 512
NC = T // CW
TC = CW // P
NPART = 3
SK = NPART * NPART * DK
SKM = SK + NPART
VW = 2 * DK
E = 8
F = 512
FC = F // P
MT = (2 * T + E * (P - 1)) // P
NEG = -3.0e38
EPS = 1e-5
JITTER2 = 2.0 * 0.01
SCALE = DK ** -0.5

UNITS = [(c, j) for c in range(NC) for j in range(TC * (c + 1))]
UNIT_AT = {u: q for q, u in enumerate(UNITS)}
MOUT0 = 16 * NC
NU = len(UNITS)
NPAIR = 2 * NU


def unit_columns(c, j):
    first = P * max(0, j - TC * c)
    return first, CW - first


def blocks(dg, s):
    return [("block", dg, i, c, h) for c in range(s + 1) for i in range(s * TC, (s + 1) * TC) for h in range(HG)]


def after(n, items, turn):
    return items[:n] + [turn] + items[n:]


TURN_LAG = 7
AHEAD_ITEMS = blocks(1, 0) + after(TURN_LAG, blocks(1, 1), ("turn", 1, 0)) + after(TURN_LAG, blocks(1, 2), ("turn", 1, 1))
REST_ITEMS = after(TURN_LAG, blocks(0, 3), ("turn", 0, 2))
FIRST_ITEMS = [(it[0], 0, *it[2:]) for it in AHEAD_ITEMS]
LOOP_ITEMS = REST_ITEMS + after(TURN_LAG, AHEAD_ITEMS, ("turn", 0, 3))
LAST_ITEMS = REST_ITEMS + [("turn", 0, 3)]
NF, NI, NL = len(FIRST_ITEMS), len(LOOP_ITEMS), len(LAST_ITEMS)


def turn_at(items, dg, s):
    return items.index(("turn", dg, s))


def last_block(items, dg, s, c=None):
    return max(n for n, it in enumerate(items)
               if it[0] == "block" and it[1] == dg and it[2] // TC == s and c in (None, it[3]))


def block_width(i, c):
    return CW if c < i // TC else P * (i % TC + 1)


def item_cost(it):
    return block_width(it[2], it[3]) + 200 if it[0] == "block" else 60


def spread(items, begin, end):
    total_u = sum(unit_columns(*u)[1] + 60 for u in UNITS)
    total_i = sum(item_cost(it) for it in items)
    share, n, done_u, done_i = [], 0, 0, 0
    for u in UNITS:
        done_u += unit_columns(*u)[1] + 60
        n0 = n
        while n < len(items) and done_i < total_i * (done_u / total_u - begin) / (end - begin):
            done_i += item_cost(items[n])
            n += 1
        share.append(n - n0)
    return share


def ranges(share):
    ends = [sum(share[:q + 1]) for q in range(NU)]
    return [(e - k, e) for e, k in zip(ends, share)]


REST_END = 0.40
FFN_BEFORE = 12
LOOP_SHARE = ranges([a + b for a, b in zip(spread(REST_ITEMS, 0.0, REST_END),
                                           spread(LOOP_ITEMS[len(REST_ITEMS):], REST_END, 1.0))])
LAST_SHARE = ranges([a + b for a, b in zip(spread(REST_ITEMS, 0.0, REST_END),
                                           spread([("turn", 0, 3)], REST_END + 0.06, 0.5))])
NO_SHARE = [(0, 0)] * NU

PIECES = [(c, 0, CW) for c in range(NC - 1)] + [(NC - 1, 0, CW // 2), (NC - 1, CW // 2, CW)]
NPC = len(PIECES)
PIECE_UNIT = [UNIT_AT[(c, TC * c + end // P - 1)] for c, _, end in PIECES]
SPREAD_AT = {20: [0], 28: [1], 33: [2]}
PROJECT_AT = {27: [0], 32: [1], 36: [2]}
GATE_AT = {9: 0, 10: 1, 11: 2, 12: 3}


def build(nc, x, wqkvT, woT, gateT, w1T, w3T, w2T, out):
    ctx = ExitStack()
    with ctx:
        def sb(name, shape, dt=F32):
            return ctx.enter_context(nc.sbuf_tensor(name, shape, dt))

        def sem(name):
            return ctx.enter_context(nc.semaphore(name))

        qparts = nc.dram_tensor("qparts", [NC, NPART, DK, H, CW], BF16, kind="Internal").ap()
        kparts = nc.dram_tensor("kparts", [NC, DK, NPART, H, CW], BF16, kind="Internal").ap()
        mparts = nc.dram_tensor("mparts", [NC, NPART, H, CW], BF16, kind="Internal").ap()
        attn_raw = nc.dram_tensor("attn_raw", [NG - 1, P, T], F32, kind="Internal").ap()
        recips = nc.dram_tensor("recips", [(NG - 1) * HG, T], F32, kind="Internal").ap()
        slot_x = nc.dram_tensor("slot_x", [MT * P, D], F32, kind="Internal").ap()
        slot_y = nc.dram_tensor("slot_y", [MT * P, D], F32, kind="Internal").ap()

        psS = ctx.enter_context(nc.psum_tensor("psS", [P, 4, CW], F32))
        psM = ctx.enter_context(nc.psum_tensor("psM", [P, 3, CW], F32))
        psO = ctx.enter_context(nc.psum_tensor("psO", [P, CW], F32))

        X = sb("X", [P, NT, D])
        xn = sb("xn", [P, NT, D])
        xnT = sb("xnT", [P, T])
        wqkv_sb = sb("wqkv_sb", [P, 3 * D])
        wo_sb = sb("wo_sb", [P, D])
        wo_last = sb("wo_last", [P, D])
        take_den = sb("take_den", [P, P])
        gate_sb = sb("gate_sb", [P, E])
        W1 = sb("W1", [P, E * F])
        W3 = sb("W3", [P, E * F])
        W2 = sb("W2", [P, E * FC * D])
        stats = sb("stats", [P, NT, 6])
        mv = sb("mv", [P, NT, 2])
        var_eps = sb("var_eps", [P, NT])
        minus_half = sb("minus_half", [P, TC])
        rstd = sb("rstd", [P, NT])
        ident = sb("ident", [P, P])
        identb = sb("identb", [P, P], BF16)
        behind = sb("behind", [P, P], BF16)
        before = sb("before", [P, P])
        ones = sb("ones", [P, P])
        causal = sb("causal", [P, CW])
        zeros = sb("zeros", [P, D])
        minus_one = sb("minus_one", [NPART, CW], BF16)
        Vp = sb("Vp", [P, NT, H, VW])
        rest = sb("rest", [P, 2, CW])
        QA = sb("QA", [P, NC, HG, CW], BF16)
        KA = sb("KA", [P, NC, HG, CW], BF16)
        QB = sb("QB", [P, NC, HG, CW], BF16)
        KB = sb("KB", [P, NC, HG, CW], BF16)
        VA = sb("VA", [P, NT, HG, VW])
        probs = sb("probs", [P, 2, HG, CW])
        junk = sb("junk", [P, 3, CW], BF16)
        QP = W2[:, :].bitcast(BF16)[:, 0:NC * NPART * CW].rearrange("p (c a n) -> p c a n", c=NC, a=NPART)
        KP = probs[:, :, :, :].rearrange("p b h n -> p (b h n)").bitcast(BF16)[:, 0:NC * NPART * CW].rearrange(
            "p (c a n) -> p c a n", c=NC, a=NPART)
        mpart = sb("mpart", [P, HG, NT, NC])
        mfull = sb("mfull", [P, NC, HG * TC])
        mrest = sb("mrest", [P, NC, HG * TC])
        msplit = sb("msplit", [P, NC, NPART, HG * TC], BF16)
        mturn = sb("mturn", [NPART * HG * TC, NC, P], BF16)
        orow = xnT[:, :].rearrange("p (c n) -> p c n", c=NC)

        x_in = [sem(f"x_in{k}") for k in range(NC)]
        w_in = sem("w_in")
        ew_in = sem("ew_in")
        cst = sem("cst")
        dve_c = sem("dve_c")
        xn_ok = sem("xn_ok")
        var_ok = sem("var_ok")
        rstd_ok = sem("rstd_ok")
        xt_ps = sem("xt_ps")
        xt_ok = sem("xt_ok")
        lg_ps = sem("lg_ps")
        v_ps = sem("v_ps")
        v_ok = sem("v_ok")
        qk_ps = sem("qk_ps")
        p1_ok = sem("p1_ok")
        r1_ok = sem("r1_ok")
        p2_ok = sem("p2_ok")
        p3_ok = sem("p3_ok")
        parts_out = [sem(f"parts_out{k}") for k in range(NC)]
        kset = sem("kset")
        kone_in = sem("kone_in")
        v_set = sem("v_set")
        wo_set = sem("wo_set")
        o_zero = sem("o_zero")
        kb_in = [sem(f"kb_in{p}") for p in range(NC)]
        qb_in = [sem(f"qb_in{p}") for p in range(NC)]
        ka_in = [sem(f"ka_in{p}") for p in range(NC)]
        qa_in = [sem(f"qa_in{p}") for p in range(NC)]
        va_in = sem("va_in")
        m_mm = sem("m_mm")
        m_red = sem("m_red")
        m_full = sem("m_full")
        m_cut = sem("m_cut")
        m_chain = sem("m_chain")
        m_out = sem("m_out")
        d_passed, p_passed, l_passed = sem("d_passed"), sem("p_passed"), sem("l_passed")
        s_mm = sem("s_mm")
        s_exp = sem("s_exp")
        o_mm = sem("o_mm")
        o_row = sem("o_row")
        o_out = sem("o_out")
        route = Route(nc, sb, sem, rest[:, :, :].rearrange("p b n -> p (b n)")[:, 0:MT * (E - 1)]
                      .rearrange("p (t e) -> p t e", e=E - 1))
        halves = [a[:, :, :, :].rearrange("p c h n -> p (c h n)").bitcast(F32) for a in (QA, KA)]
        ffn = Ffn(nc, sb, sem, probs[:, :, :, :].rearrange("p b h n -> p (b h) n"), route, (W1, W3, W2), halves)
        fin = Final(nc, sem, W1, W3, W2, Vp, orow, wo_sb, wo_last, take_den, rest)
        fin.m_red = ffn.m_red = m_red

        def group(g):
            return bass.ds(g * HG, HG)

        block = ctx.enter_context(nc.Block())

        @block.sync
        def _(sp):
            def load_k(dst, g, p, done):
                sp.dma_start(dst[0:SK, p, :, :].rearrange("r h n -> r (h n)"),
                             kparts[p, :, :, group(g), :].rearrange("k j h n -> (k j) (h n)").unsqueeze(0)
                             .to_broadcast([NPART, NPART * DK, HG * CW])).then_inc(done, 16)

            def load_q(dst, g, p, done):
                sp.dma_start(dst[0:SK, p, :, :].rearrange("r h n -> r (h n)"),
                             qparts[p, :, :, group(g), :].rearrange("i k h n -> (i k) (h n)").unsqueeze(1)
                             .to_broadcast([NPART * DK, NPART, HG * CW])).then_inc(done, 16)

            def load_m(g, p, done):
                sp.dma_start(QA[SK:SKM, p, :, :].rearrange("a h n -> a (h n)"),
                             mparts[p, :, group(g), :].rearrange("a h n -> a (h n)")).then_inc(done, 16)

            def store_m(g, s):
                sp.dma_start(mparts[s, :, group(g), :].rearrange("a h (i n) -> a (h i) n", n=P),
                             mturn[:, s, :]).then_inc(m_out, 16)

            def store_o(g, c):
                sp.dma_start(attn_raw[bass.ds(g, 1), :, c * CW:(c + 1) * CW].rearrange("a p n -> (a p) n"),
                             orow[:, c, :]).then_inc(o_out, 16)

            sp.sem_inc(o_out, 1)
            sp.sem_inc(m_out, MOUT0)
            for k in range(NC):
                sp.dma_start(X[:, TC * k:TC * (k + 1), :],
                             x[k * CW:(k + 1) * CW, :].rearrange("(i p) d -> p i d", p=P)).then_inc(x_in[k], 16)
            sp.wait_ge(route.zeroed, 1)
            sp.dma_start(slot_x.rearrange("(i p) d -> p i d", p=P),
                         zeros[:, :].unsqueeze(1).to_broadcast([P, MT, D])).then_inc(route.filled, 16)
            sp.wait_ge(wo_set, 1)
            fin.sp_weights(sp, woT)
            for k in range(NC + 1):
                if k < NC:
                    sp.wait_ge(p3_ok, 2 * k + 1)
                    for j in range(NPART):
                        sp.dma_start(kparts[k, :, j, :, :], KP[:, k, j, :]).then_inc(parts_out[k], 16)
                    sp.wait_ge(p3_ok, 2 * k + 2)
                    sp.dma_start(qparts[k].rearrange("i k h n -> (k h) i n"), QP[:, k, :, :]
                                 ).then_inc(parts_out[k], 16)
                if k:
                    sp.wait_ge(parts_out[k - 1], 64)
                    load_k(KB, 0, k - 1, kb_in[k - 1])
                    load_q(QB, 0, k - 1, qb_in[k - 1])
            for s in range(NC - 1):
                if s == NC - 2:
                    ffn.sp_first(sp, slot_x, route)
                sp.wait_ge(m_mm, last_block(FIRST_ITEMS, 0, s) + 1)
                load_q(QB, 1, s, qb_in[s])
                if s:
                    sp.wait_ge(m_red, turn_at(FIRST_ITEMS, 0, s - 1) + 1)
                    store_m(0, s - 1)

            def first_stacks():
                sp.wait_ge(m_out, MOUT0 + 16 * (NC - 2))
                sp.wait_ge(kset, 1)
                sp.dma_start(KA[SK:SKM, :, :, :].rearrange("a c h n -> a (c h) n"),
                             minus_one[:, :].unsqueeze(1).to_broadcast([NPART, NC * HG, CW])).then_inc(kone_in, 16)
                for p in range(NC):
                    load_k(KA, 0, p, ka_in[p])
                    load_q(QA, 0, p, qa_in[p])
                    if p < NC - 2:
                        load_m(0, p, qa_in[p])

            ffn.sp(sp, slot_x, slot_y, first_stacks)

            def unit_scores(g, c, j):
                sp.wait_ge(s_mm, NPAIR * g + 2 * UNIT_AT[(c, j)] + 2)

            def item_turned(g, items, dg, s):
                sp.wait_ge(m_red, NF + NI * g + turn_at(items, dg, s) + 1)
                store_m(g + dg, s)
                sp.wait_ge(m_out, MOUT0 + (g + dg) * (16 * NC) + 16 * (s + 1))
                load_m(g + dg, s, qa_in[s])

            def item_blocks(g, dg, s, c=None):
                sp.wait_ge(m_mm, NF + NI * g + last_block(LOOP_ITEMS, dg, s, c) + 1)

            def sums_out(g, c):
                sp.wait_ge(o_row, NC * g + c + 2)
                store_o(g, c)

            with sp.Fori(0, NG - 1) as g:
                nxt = (g + 2) % NG
                item_turned(g, LOOP_ITEMS, 0, 2)
                unit_scores(g, 0, TC - 1)
                load_q(QA, g + 1, 0, qa_in[0])
                sums_out(g, 0)
                item_blocks(g, 0, 3, 0)
                load_k(KB, g + 1, 0, kb_in[0])
                item_blocks(g, 0, 3, 1)
                load_k(KB, g + 1, 1, kb_in[1])
                unit_scores(g, 1, 2 * TC - 1)
                load_q(QA, g + 1, 1, qa_in[1])
                sums_out(g, 1)
                item_blocks(g, 0, 3, 2)
                load_k(KB, g + 1, 2, kb_in[2])
                item_blocks(g, 0, 3, 3)
                load_k(KB, g + 1, 3, kb_in[3])
                load_q(QB, g + 1, 3, qb_in[3])
                item_turned(g, LOOP_ITEMS, 0, 3)
                item_blocks(g, 1, 0)
                load_q(QB, nxt, 0, qb_in[0])
                item_turned(g, LOOP_ITEMS, 1, 0)
                unit_scores(g, 2, 3 * TC - 1)
                load_q(QA, g + 1, 2, qa_in[2])
                sums_out(g, 2)
                unit_scores(g, 3, TC - 1)
                load_k(KA, g + 1, 0, ka_in[0])
                item_blocks(g, 1, 1)
                load_q(QB, nxt, 1, qb_in[1])
                item_turned(g, LOOP_ITEMS, 1, 1)
                unit_scores(g, 3, 2 * TC - 1)
                load_k(KA, g + 1, 1, ka_in[1])
                unit_scores(g, 3, 3 * TC - 1)
                load_k(KA, g + 1, 2, ka_in[2])
                item_blocks(g, 1, 2)
                load_q(QB, nxt, 2, qb_in[2])
                unit_scores(g, 3, 4 * TC - 1)
                load_k(KA, g + 1, 3, ka_in[3])
                load_q(QA, g + 1, 3, qa_in[3])
                sums_out(g, 3)

            g = NG - 1
            item_turned(g, LAST_ITEMS, 0, 2)
            sp.wait_ge(o_out, 16 * (NG - 1) * NC + 1)
            sp.wait_ge(va_in, NG * NC)
            fin.sp_sums(sp, attn_raw)
            item_turned(g, LAST_ITEMS, 0, 3)
            for p in range(NC - 1):
                sp.wait_ge(qb_in[p], 16 * (NG + 1))
            fin.sp_recips(sp, recips)
            fin.sp_out(sp, out)

        @block.gpsimd
        def _(pool):
            nc.gpsimd.memset(ident[:, :], 0.0).then_inc(cst, 1)
            nc.gpsimd.memset(ones[:, :], 1.0).then_inc(cst, 1)
            nc.gpsimd.memset(causal[:, :], 0.0).then_inc(cst, 1)
            nc.gpsimd.memset(minus_one[:, :], -1.0).then_inc(kset, 1)
            nc.gpsimd.memset(zeros[:, :], 0.0).then_inc(route.zeroed, 1)
            nc.gpsimd.memset(wo_last[:, :], 0.0).then_inc(wo_set, 1)
            nc.gpsimd.memset(minus_half[:, :], -0.5).then_inc(cst, 1)
            pool.wait_ge(cst, 4)
            nc.gpsimd.affine_select(out=ident[:, :], in_=ident[:, :], compare_op=ALU.not_equal, fill=1.0,
                                    base=0, pattern=[[-1, P]], channel_multiplier=1).then_inc(cst, 1)
            nc.gpsimd.affine_select(out=before[:, :], in_=ones[:, :], compare_op=ALU.is_gt, fill=0.0,
                                    base=0, pattern=[[1, P]], channel_multiplier=-1).then_inc(cst, 1)
            nc.gpsimd.affine_select(out=causal[:, CW - P:], in_=causal[:, CW - P:], compare_op=ALU.is_ge, fill=NEG,
                                    base=0, pattern=[[-1, P]], channel_multiplier=1).then_inc(cst, 1)
            pool.wait_ge(cst, 5)
            nc.gpsimd.tensor_copy(identb[:, :], ident[:, :]).then_inc(cst, 1)
            nc.gpsimd.tensor_copy(take_den[:, :].rearrange("p (h r) -> p h r", h=HG),
                                  ident[:, :].rearrange("p (h r) -> p h r", h=HG)[:, :, DK:DK + 1]
                                  .to_broadcast([P, HG, P // HG])).then_inc(cst, 1)
            nc.gpsimd.memset(behind[:, :], 0.0).then_inc(cst, 1)
            pool.wait_ge(cst, 10)
            nc.gpsimd.affine_select(out=behind[:, :], in_=behind[:, :], compare_op=ALU.is_ge, fill=NEG,
                                    base=0, pattern=[[1, P]], channel_multiplier=-1).then_inc(cst, 1)
            for k in range(NC):
                pool.wait_ge(var_ok, k + 1)
                nc.gpsimd.tensor_tensor(rstd[:, TC * k:TC * k + TC], var_eps[:, TC * k:TC * k + TC],
                                        minus_half[:, 0:TC], ALU.pow).then_inc(rstd_ok, 1)
            route.pool_constants(pool)
            for n in range(2 * NC):
                dst = (KP, QP)[n % 2]
                pool.wait_ge(p2_ok, n + 1)
                nc.gpsimd.tensor_tensor(dst[:, n // 2, 2, :], rest[:, n % 2, :], dst[:, n // 2, 1, :],
                                        ALU.subtract).then_inc(p3_ok, 1)

            def place_v(g, p):
                nc.gpsimd.tensor_copy(VA[:, p * TC:(p + 1) * TC, :, :],
                                      Vp[:, p * TC:(p + 1) * TC, group(g), :]).then_inc(va_in, 1)

            def cut_maxima(gm, s):
                wait_apart(pool, m_full, gm * NC + s + 1, l_passed)
                nc.gpsimd.tensor_copy(msplit[:, s, 0, :], mfull[:, s, :]).then_inc(m_chain, 1)
                pool.wait_ge(m_chain, gm * (3 * NC) + 3 * s + 1)
                nc.gpsimd.tensor_tensor(mrest[:, s, :], mfull[:, s, :], msplit[:, s, 0, :],
                                        ALU.subtract).then_inc(m_chain, 1)
                wait_apart(pool, m_chain, gm * (3 * NC) + 3 * s + 2, l_passed)
                nc.gpsimd.tensor_copy(msplit[:, s, 1, :], mrest[:, s, :]).then_inc(m_chain, 1)
                pool.wait_ge(m_chain, gm * (3 * NC) + 3 * s + 3)
                nc.gpsimd.tensor_tensor(msplit[:, s, 2, :], mrest[:, s, :], msplit[:, s, 1, :],
                                        ALU.subtract).then_inc(m_cut, 1)

            route.pool_slots(pool)
            n = 0
            for s, upto in enumerate((5, 18, 2 * NT)):
                while n < upto:
                    route.scatter(pool, xn, slot_x, n)
                    n += 1
                if s == NC - 2:
                    ffn.pool_split(pool)
                    pool.wait_ge(v_set, 1)
                    for p in range(NC):
                        pool.wait_ge(v_ok, p + 1)
                        place_v(0, p)
                cut_maxima(0, s)
            ffn.pool(pool)
            for n in range(2 * NT):
                fin.gather(pool, route, slot_y, n)

            with pool.Fori(0, NG - 1) as g:
                cut_maxima(g, NC - 1)
                cut_maxima(g + 1, 0)
                cut_maxima(g + 1, 1)
                for p in range(NC):
                    if p == NC - 1:
                        cut_maxima(g + 1, 2)
                    wait_apart(pool, o_mm, NU * g + UNIT_AT[(NC - 1, TC * p + TC - 1)] + 1, l_passed)
                    place_v(g + 1, p)
            fin.pool_mix(pool, route)
            fin.pool_gate_den(pool)
            cut_maxima(NG - 1, NC - 1)
            fin.pool_gate(pool)

        @block.scalar
        def _(act):
            act.sem_inc(o_row, 1)
            act.dma_start(wqkv_sb[:, :], wqkvT).then_inc(w_in, 16)
            act.dma_start(gate_sb[:, :], gateT).then_inc(w_in, 16)
            act.dma_start(wo_sb[:, :], woT).then_inc(w_in, 16)
            def tokens_out(k):
                act.wait_ge(xt_ps, k + 1)
                nc.scalar.activation(xnT[:, k * CW:(k + 1) * CW], psS[:, k, :], ACT.Copy).then_inc(xt_ok, 1)

            def two_parts(n):
                dst = (KP, QP)[n % 2]
                act.wait_ge(qk_ps, n + 1)
                nc.scalar.activation(dst[:, n // 2, 0, :], psM[:, n % 3, :], ACT.Copy).then_inc(p1_ok, 1)
                act.wait_ge(r1_ok, n + 1)
                nc.scalar.activation(dst[:, n // 2, 1, :], rest[:, n % 2, :], ACT.Copy).then_inc(p2_ok, 1)

            def values_out(k):
                act.wait_ge(v_ps, k + 1)
                nc.scalar.activation(Vp[:, k * TC:(k + 1) * TC, :, 0:DK],
                                     psS[:, k, :].rearrange("p (j h w) -> p j h w", j=TC, h=H),
                                     ACT.Copy).then_inc(v_ok, 1)

            tokens_out(0)
            tokens_out(1)
            two_parts(0)
            two_parts(1)
            tokens_out(2)
            tokens_out(3)
            for k in range(NC):
                if k:
                    two_parts(2 * k)
                    two_parts(2 * k + 1)
                values_out(k)
                if k == 2:
                    route.act(act)
            act.wait_ge(m_mm, 4)
            act.dma_start(W1[:, :].rearrange("p (e f) -> p e f", e=E), w1T.rearrange("e p f -> p e f")).then_inc(ew_in, 16)
            act.wait_ge(m_mm, 20)
            act.dma_start(W3[:, :].rearrange("p (e f) -> p e f", e=E), w3T.rearrange("e p f -> p e f")).then_inc(ew_in, 16)
            act.wait_ge(m_mm, 40)
            for p in range(NC):
                act.wait_ge(parts_out[p], 64)
            for e in range(E):
                act.dma_start(W2[:, e * FC * D:(e + 1) * FC * D].rearrange("p (c d) -> p c d", c=FC),
                              w2T[e].rearrange("(c p) d -> p c d", p=P)).then_inc(ew_in, 16)

            def evacuate(g, c, first=0, end=CW, bank=psO):
                act.wait_ge(o_mm, g * NU + UNIT_AT[(c, TC * c + end // P - 1)] + 1)
                act.wait_ge(o_out, g * (16 * NC) + 1)
                nc.scalar.activation(orow[:, c, first:end], bank[:, first:end], ACT.Copy).then_inc(o_row, 1)

            def exps(g, last=False):
                for q, (c, j) in enumerate(UNITS):
                    if last and q in GATE_AT:
                        fin.act(act, GATE_AT[q])
                    if last and q == NU - 1:
                        evacuate(g, NC - 1, 0, CW // 2, psM[:, 1, :])
                    first, w = unit_columns(c, j)
                    for p in range(2):
                        act.wait_ge(s_mm, g * NPAIR + 2 * q + p + 1)
                        if p == 0 and q >= 2:
                            act.wait_ge(o_mm, g * NU + q - 1)
                        nc.scalar.activation(probs[:, q % 2, 2 * p:2 * p + 2, 0:w], psS[:, 2 * p:2 * p + 2, 0:w],
                                             ACT.Exp, scale=SCALE).then_inc(s_exp, 1)
                        if p == 0 and j == 0 and c > 0:
                            evacuate(g, c - 1)
                evacuate(g, NC - 1, CW // 2 if last else 0)

            act.wait_ge(ew_in, 16 * (2 + E))
            ffn.act_split(act)
            step = ffn.act_step(act, psS, psM, psO)
            ffn.early(step)
            ffn.steps(act, step)
            with act.Fori(0, NG - 1) as g:
                exps(g)
            exps(NG - 1, last=True)

        @block.vector
        def _(dve):
            chain = [0]

            def link(ins):
                chain[0] += 1
                ins.then_inc(dve_c, 1)
                dve.wait_ge(dve_c, chain[0])

            def normalise(k):
                dve.wait_ge(rstd_ok, k + 1)
                for i in range(TC * k, TC * k + TC):
                    last = nc.vector.tensor_scalar(xn[:, i, :], X[:, i, :], mv[:, i, 0:1], rstd[:, i:i + 1],
                                                   ALU.subtract, ALU.mult)
                last.then_inc(xn_ok, 1)

            nc.vector.memset(mpart[:, :, :, :], NEG)
            nc.vector.memset(psO[:, :], 0.0).then_inc(o_zero, 1)
            nc.vector.memset(Vp[:, :, :, DK:], 1.0).then_inc(v_set, 1)
            for k in range(NC):
                dve.wait_ge(x_in[k], 16)
                for i in range(TC * k, TC * k + TC):
                    last = nc.vector.bn_stats(stats[:, i, :], X[:, i, :])
                link(last)
                for i in range(TC * k, TC * k + TC):
                    last = nc.vector.bn_aggr(mv[:, i, :], stats[:, i, :])
                link(last)
                nc.vector.tensor_scalar(var_eps[:, TC * k:TC * k + TC], mv[:, TC * k:TC * k + TC, 1], EPS, None,
                                        ALU.add).then_inc(var_ok, 1)
                if k:
                    normalise(k - 1)
            normalise(NC - 1)
            for n in range(2 * NC):
                dst = (KP, QP)[n % 2]
                dve.wait_ge(p1_ok, n + 1)
                if n >= 2:
                    dve.wait_ge(p3_ok, n - 1)
                nc.vector.tensor_tensor(rest[:, n % 2, :], psM[:, n % 3, :], dst[:, n // 2, 0, :],
                                        ALU.subtract).then_inc(r1_ok, 1)
                if n == 3:
                    route.dve_first(dve, link, psO, lg_ps)
                elif n == 4:
                    route.dve_second(link)
                elif n == 5:
                    route.dve_distances(link)
            route.dve_slots(dve, link, psO, p3_ok)

            def max_item(base, g, items, n):
                it = items[n]
                gm = g + it[1]
                if it[0] == "block" and it[3] == it[2] // TC:
                    wait_apart(dve, m_mm, base + n + 1, d_passed)
                else:
                    dve.wait_ge(m_mm, base + n + 1)
                if it[0] == "turn":
                    dve.wait_ge(m_out, gm * (16 * NC) + 16 * (it[2] + 1))
                    nc.vector.tensor_copy(mturn[:, it[2], :], psM[:, n % 3, :].bitcast(BF16)[0:NPART * HG * TC, 0:P]
                                          ).then_inc(m_red, 1)
                    return
                _, _, i, c, h = it
                w = block_width(i, c)
                if c < i // TC:
                    nc.vector.tensor_reduce(out=mpart[:, h, i, c:c + 1], in_=psM[:, n % 3, :], axis=AX.X,
                                            op=ALU.max).then_inc(m_red, 1)
                else:
                    nc.vector.tensor_tensor_reduce(
                        out=junk[:, n % 3, 0:w], in0=psM[:, n % 3, 0:w], in1=causal[:, CW - w:], scale=1.0, scalar=NEG,
                        op0=ALU.add, op1=ALU.max, accum_out=mpart[:, h, i, c:c + 1]).then_inc(m_red, 1)
                s = i // TC
                if n == last_block(items, it[1], s):
                    dve.wait_ge(m_red, base + n + 1)
                    nc.vector.tensor_reduce(out=mfull[:, s, :].rearrange("p (h i) -> p h i", h=HG),
                                            in_=mpart[:, :, s * TC:(s + 1) * TC, :], axis=AX.X,
                                            op=ALU.max).then_inc(m_full, 1)

            step = ffn.dve_step(dve, link, psS, psM, psO)
            for n in range(NF - FFN_BEFORE):
                max_item(0, 0, FIRST_ITEMS, n)
            ffn.early(step)
            for n in range(NF - FFN_BEFORE, NF):
                max_item(0, 0, FIRST_ITEMS, n)
            ffn.steps(dve, step)
            with dve.Fori(0, NG - 1) as g:
                for n in range(NI):
                    max_item(g * NI + NF, g, LOOP_ITEMS, n)
            for n in range(NL):
                max_item(NF + (NG - 1) * NI, NG - 1, LAST_ITEMS, n)
            fin.dve(dve, link, psM, psS, X)

        @block.tensor
        def _(pe):
            pe.wait_ge(cst, 11)
            def turn_tokens(k):
                pe.wait_ge(xn_ok, k + 1)
                for i in range(TC):
                    last = nc.tensor.transpose(psS[:, k, i * P:(i + 1) * P], xn[:, k * TC + i, :], ident[:, :])
                last.then_inc(xt_ps, 1)

            def project_tokens(k):
                pe.wait_ge(xt_ok, k + 1)
                for w in range(2):
                    n = 2 * k + w
                    if n >= 3:
                        pe.wait_ge(r1_ok, n - 2)
                    nc.tensor.matmul(psM[:, n % 3, :], wqkv_sb[:, (1 - w) * D:(2 - w) * D],
                                     xnT[:, k * CW:(k + 1) * CW], start=True, stop=True).then_inc(qk_ps, 1)
                for i in range(TC):
                    last = nc.tensor.matmul(psS[:, k, i * D:(i + 1) * D], xnT[:, k * CW + i * P:k * CW + (i + 1) * P],
                                            wqkv_sb[:, 2 * D:3 * D], start=True, stop=True)
                last.then_inc(v_ps, 1)

            turn_tokens(0)
            turn_tokens(1)
            pe.wait_ge(w_in, 48)
            project_tokens(0)
            turn_tokens(2)
            turn_tokens(3)
            project_tokens(1)
            pe.wait_ge(xt_ok, NC)
            pe.wait_ge(o_zero, 1)
            for i in range(NT):
                last = nc.tensor.matmul(psO[:, i * E:(i + 1) * E], xnT[:, i * P:(i + 1) * P], gate_sb[:, :],
                                        start=True, stop=True)
            last.then_inc(lg_ps, 1)
            project_tokens(2)
            project_tokens(3)
            route.pe(pe, psO, before, ones)

            def max_item(base, g, items, n):
                it = items[n]
                gm = g + it[1]
                if n >= 3:
                    pe.wait_ge(m_red, base + n - 2)
                elif not (isinstance(base, int) and base == 0):
                    pe.wait_ge(m_red, base)
                if it[0] == "turn":
                    s = it[2]
                    wait_apart(pe, m_cut, gm * NC + s + 1, p_passed)
                    nc.tensor.transpose(psM[:, n % 3, :].bitcast(BF16)[0:NPART * HG * TC, 0:P],
                                        msplit[:, s, :, :].rearrange("p a m -> p (a m)"), identb[:, :]
                                        ).then_inc(m_mm, 1)
                    return
                _, _, i, c, h = it
                if i % TC == 0 and h == 0:
                    if c == 0:
                        pe.wait_ge(qb_in[i // TC], gm * 16 + 16)
                    if c == i // TC:
                        pe.wait_ge(kb_in[c], gm * 16 + 16)
                w = block_width(i, c)
                nc.tensor.matmul(psM[:, n % 3, 0:w], QB[0:SK, i // TC, h, i % TC * P:(i % TC + 1) * P],
                                 KB[0:SK, c, h, 0:w], start=True, stop=True).then_inc(m_mm, 1)

            def scores(g, q, p):
                c, j = UNITS[q]
                first, w = unit_columns(c, j)
                if q >= 1:
                    pe.wait_ge(s_exp, g * NPAIR + 2 * q + p - 1)
                if j == 0 and p == 0:
                    pe.wait_ge(qa_in[c], g * 32 + 32)
                if j == TC * c and p == 0:
                    pe.wait_ge(ka_in[c], g * 16 + 16)
                for u in range(2):
                    h = 2 * p + u
                    last = nc.tensor.matmul(psS[:, h, 0:w], KA[0:SKM, j // TC, h, j % TC * P:(j % TC + 1) * P],
                                            QA[0:SKM, c, h, first:CW],
                                            start=True, stop=j < TC * c)
                    if j >= TC * c:
                        last = nc.tensor.matmul(psS[:, h, 0:P], identb[:, :], behind[:, :], start=False, stop=True)
                last.then_inc(s_mm, 1)

            def weigh(g, q, halves=False):
                c, j = UNITS[q]
                first, w = unit_columns(c, j)
                pe.wait_ge(s_exp, g * NPAIR + 2 * q + 2)
                if j == TC * c:
                    pe.wait_ge(va_in, g * NC + c + 1)
                if j == 0:
                    pe.wait_ge(o_row, g * NC + c + 1)
                if halves and j == 0:
                    pe.wait_ge(fin.left_zero, 1)
                parts = ((psM[:, 1, :], 0, CW // 2), (psO, CW // 2, CW)) if halves else ((psO, 0, CW),)
                for bank, lo, hi in parts:
                    lo = max(lo, first)
                    for h in range(HG if lo < hi else 0):
                        last = nc.tensor.matmul(bank[32 * h:32 * h + VW, lo:hi], VA[:, j, h, :],
                                                probs[:, q % 2, h, lo - first:hi - first],
                                                start=(j == 0), stop=(j == TC * c + hi // P - 1))
                last.then_inc(o_mm, 1)

            def attention(g, items, share, last=False):
                base = g * NI + NF
                for q in range(NU):
                    n0, n1 = share[q]
                    cuts = [n0 + (n1 - n0) * k // 3 for k in range(4)]
                    if last:
                        for k in SPREAD_AT.get(q, ()):
                            fin.spread(pe, k, psM, o_row)
                        for k in PROJECT_AT.get(q, ()):
                            fin.project(pe, k, psM, psS)
                    scores(g, q, 0)
                    for n in range(cuts[0], cuts[1]):
                        max_item(base, g, items, n)
                    scores(g, q, 1)
                    for n in range(cuts[1], cuts[2]):
                        max_item(base, g, items, n)
                    if q:
                        weigh(g, q - 1, last and q > UNIT_AT[(NC - 1, 0)])
                    for n in range(cuts[2], cuts[3]):
                        max_item(base, g, items, n)
                if last:
                    fin.spread(pe, 3, psM, o_row)
                weigh(g, NU - 1, last)

            pe.wait_ge(v_ok, NC)
            pe.wait_ge(o_zero, 1)
            step = ffn.pe_step(pe, ident, psS, psM, psO)
            for n in range(NF - FFN_BEFORE):
                max_item(0, 0, FIRST_ITEMS, n)
            pe.wait_ge(route.slots_ok, 3)
            ffn.early(step)
            for n in range(NF - FFN_BEFORE, NF):
                max_item(0, 0, FIRST_ITEMS, n)
            pe.wait_ge(ew_in, 16 * (2 + E))
            ffn.steps(pe, step, before_loop=lambda: pe.wait_ge(ffn.w_ok, E))
            ffn.pe_end(pe)
            pe.wait_ge(kone_in, 16)
            with pe.Fori(0, NG - 1) as g:
                attention(g, LOOP_ITEMS, LOOP_SHARE)
            attention(NG - 1, LAST_ITEMS, LAST_SHARE, last=True)
            fin.spread(pe, 4, psM, o_row)
            fin.project(pe, 3, psM, psS)
            fin.project(pe, 4, psM, psS)


def wait_apart(eng, sem, value, passed):
    eng.wait_ge(sem, value)
    if not isinstance(value, int):
        eng.sem_inc(passed, 1)


def whole(t):
    return t[:, :, :]


class Route:

    def __init__(self, nc, sb, sem, tcmp):
        self.nc = nc
        t = lambda name, dt=F32: sb("rt_" + name, [P, NT, E], dt)
        self.L, self.L2, self.oh1, self.oh2, self.oh = t("L"), t("L2"), t("oh1"), t("oh2"), t("oh")
        self.key, self.absl, self.d1, self.d2 = t("key"), t("absl"), t("d1"), t("d2")
        self.fac, self.keep, self.e1, self.e2 = t("fac"), t("keep"), t("e1"), t("e2")
        self.desc = sb("rt_desc", [P, E])
        self.m1, self.m2, self.k1, self.k2 = (sb(f"rt_{n}", [P, NT]) for n in ("m1", "m2", "k1", "k2"))
        self.s1, self.s2, self.w1, self.w2 = (sb(f"rt_{n}", [P, NT]) for n in ("s1", "s2", "w1", "w2"))
        self.cum = [sb(f"rt_cum{b}", [P, 8 + NT, E]) for b in range(2)]
        self.pre = t("pre")
        self.tot = t("tot")
        self.slot = t("slot")
        self.over = sb("rt_over", [P, E, NT])
        self.steps = sb("rt_steps", [P, NT])
        self.tiles = [sb(f"rt_tiles{b}", [P, 4 + E]) for b in range(2)]
        self.ntile = sb("rt_ntile", [P, E])
        self.base = sb("rt_base", [P, E])
        self.sf = [sb(f"rt_sf{b}", [P, NT]) for b in range(2)]
        self.si = [sb(f"rt_si{b}", [P, NT], I32) for b in range(2)]
        self.tau = sb("rt_tau", [P, MT])
        self.tcmp = tcmp
        self.texp = sb("rt_texp", [P, MT])
        self.tile_expert = sb("rt_tile_expert", [P, MT], I32)
        self.tile_cols = sb("rt_tile_cols", [P, MT], I32)
        self.zeroed = sem("rt_zeroed")
        self.filled = sem("rt_filled")
        self.cst = sem("rt_cst")
        self.d_ok = sem("rt_d_ok")
        self.e_ok = sem("rt_e_ok")
        self.oh_ok = sem("rt_oh_ok")
        self.pre_ps = sem("rt_pre_ps")
        self.slots_ok = sem("rt_slots_ok")
        self.scattered = sem("rt_scattered")

    def pool_constants(self, pool):
        nc = self.nc
        nc.gpsimd.iota(self.desc[:, :], [[-1, E]], base=E, channel_multiplier=0,
                       allow_small_or_imprecise_dtypes=True).then_inc(self.cst, 1)
        nc.gpsimd.iota(self.steps[:, :], [[P, NT]], base=0, channel_multiplier=0,
                       allow_small_or_imprecise_dtypes=True).then_inc(self.cst, 1)
        nc.gpsimd.iota(self.tau[:, :], [[1, MT]], base=0, channel_multiplier=0,
                       allow_small_or_imprecise_dtypes=True).then_inc(self.cst, 1)

    def act(self, act):
        act.wait_ge(self.d_ok, 1)
        self.nc.scalar.activation(self.e1[:, :, :], self.d1[:, :, :], ACT.Exp, scale=-1.0).then_inc(self.e_ok, 1)
        act.wait_ge(self.d_ok, 2)
        self.nc.scalar.activation(self.e2[:, :, :], self.d2[:, :, :], ACT.Exp, scale=-1.0).then_inc(self.e_ok, 1)

    def pe(self, pe, psO, before, ones):
        nc = self.nc
        pe.wait_ge(self.oh_ok, 1)
        ohf = self.oh[:, :, :].rearrange("p i e -> p (i e)")
        nc.tensor.matmul(psO[:, 128:256], before[:, :], ohf, start=True, stop=True)
        nc.tensor.matmul(psO[:, 256:384], ones[:, :], ohf, start=True, stop=True).then_inc(self.pre_ps, 1)

    @staticmethod
    def over_e(t):
        return t[:, :].unsqueeze(2).to_broadcast([P, NT, E])

    def dve_first(self, dve, link, psO, lg_ps):
        v, A, over_e = self.nc.vector, whole, self.over_e
        desc = self.desc[:, :].unsqueeze(1).to_broadcast([P, NT, E])
        dve.wait_ge(lg_ps, 1)
        dve.wait_ge(self.cst, 3)
        for t in (*self.cum, *self.tiles):
            v.memset(t[:, :, :] if len(t.shape) == 3 else t[:, :], 0.0)
        link(v.tensor_copy(A(self.L), psO[:, 0:NT * E].rearrange("p (i e) -> p i e", e=E)))
        link(v.tensor_reduce(out=self.m1[:, :], in_=A(self.L), axis=AX.X, op=ALU.max))
        link(v.tensor_tensor(A(self.key), A(self.L), over_e(self.m1), ALU.is_equal))
        link(v.tensor_tensor(A(self.key), A(self.key), desc, ALU.mult))
        link(v.tensor_reduce(out=self.k1[:, :], in_=A(self.key), axis=AX.X, op=ALU.max))
        link(v.tensor_tensor(A(self.oh1), over_e(self.k1), desc, ALU.is_equal))

    def dve_second(self, link):
        v, A, over_e = self.nc.vector, whole, self.over_e
        desc = self.desc[:, :].unsqueeze(1).to_broadcast([P, NT, E])
        link(v.scalar_tensor_tensor(out=A(self.L2), in0=A(self.oh1), scalar=NEG, in1=A(self.L),
                                    op0=ALU.mult, op1=ALU.add))
        link(v.tensor_reduce(out=self.m2[:, :], in_=A(self.L2), axis=AX.X, op=ALU.max))
        link(v.tensor_tensor(A(self.key), A(self.L2), over_e(self.m2), ALU.is_equal))
        link(v.tensor_tensor(A(self.key), A(self.key), desc, ALU.mult))
        link(v.tensor_reduce(out=self.k2[:, :], in_=A(self.key), axis=AX.X, op=ALU.max))
        link(v.tensor_tensor(A(self.oh2), over_e(self.k2), desc, ALU.is_equal))
        v.tensor_tensor(A(self.oh), A(self.oh1), A(self.oh2), ALU.add).then_inc(self.oh_ok, 1)

    def dve_distances(self, link):
        v, A, over_e = self.nc.vector, whole, self.over_e
        v.tensor_tensor(A(self.d1), over_e(self.m1), A(self.L), ALU.subtract).then_inc(self.d_ok, 1)
        v.scalar_tensor_tensor(out=A(self.absl), in0=A(self.L), scalar=-1.0, in1=A(self.L), op0=ALU.mult, op1=ALU.max)
        link(v.tensor_tensor(A(self.key), over_e(self.m2), A(self.L), ALU.subtract))
        v.tensor_scalar(A(self.d2), A(self.key), 0.0, None, ALU.max).then_inc(self.d_ok, 1)

    def dve_weight1(self, dve, link):
        v, A, over_e = self.nc.vector, whole, self.over_e
        link(v.tensor_tensor(A(self.fac), A(self.absl), over_e(self.m1), ALU.max))
        link(v.scalar_tensor_tensor(out=A(self.keep), in0=A(self.fac), scalar=JITTER2, in1=A(self.d1),
                                    op0=ALU.mult, op1=ALU.is_ge))
        dve.wait_ge(self.e_ok, 1)
        link(v.tensor_tensor(A(self.keep), A(self.keep), A(self.e1), ALU.mult))
        link(v.tensor_reduce(out=self.s1[:, :], in_=A(self.keep), axis=AX.X, op=ALU.add))
        v.reciprocal(self.w1[:, :], self.s1[:, :])

    def dve_weight2(self, dve, link):
        v, A, over_e = self.nc.vector, whole, self.over_e
        link(v.tensor_tensor(A(self.fac), A(self.absl), over_e(self.m2), ALU.max))
        link(v.scalar_tensor_tensor(out=A(self.keep), in0=A(self.fac), scalar=JITTER2, in1=A(self.key),
                                    op0=ALU.mult, op1=ALU.is_ge))
        link(v.tensor_tensor(A(self.keep), A(self.keep), A(self.oh1), ALU.is_gt))
        dve.wait_ge(self.e_ok, 2)
        link(v.tensor_tensor(A(self.keep), A(self.keep), A(self.e2), ALU.mult))
        link(v.tensor_reduce(out=self.s2[:, :], in_=A(self.keep), axis=AX.X, op=ALU.add))
        link(v.reciprocal(self.w2[:, :], self.s2[:, :]))

    def dve_slots(self, dve, link, psO, p3_ok):
        v, A = self.nc.vector, whole
        dve.wait_ge(self.pre_ps, 1)
        link(v.tensor_copy(A(self.pre), psO[:, 128:256].rearrange("p (i e) -> p i e", e=E)))
        link(v.tensor_copy(A(self.tot), psO[:, 256:384].rearrange("p (i e) -> p i e", e=E)))
        link(v.tensor_copy(self.cum[0][:, 8:, :], A(self.tot)))
        b = 0
        for k in (1, 2, 4, 8):
            link(v.tensor_tensor(self.cum[1 - b][:, 8:, :], self.cum[b][:, 8:, :], self.cum[b][:, 8 - k:8 + NT - k, :],
                                 ALU.add))
            b = 1 - b
        cum = self.cum[b]
        count = cum[:, 8 + NT - 1, :]
        link(v.tensor_tensor(self.over[:, :, :], count.unsqueeze(2).to_broadcast([P, E, NT]),
                             self.steps[:, :].unsqueeze(1).to_broadcast([P, E, NT]), ALU.is_gt))
        link(v.tensor_reduce(out=self.ntile[:, :], in_=self.over[:, :, :], axis=AX.X, op=ALU.add))
        link(v.tensor_copy(self.tiles[0][:, 4:], self.ntile[:, :]))
        t = 0
        for k in (1, 2, 4):
            link(v.tensor_tensor(self.tiles[1 - t][:, 4:], self.tiles[t][:, 4:], self.tiles[t][:, 4 - k:4 + E - k], ALU.add))
            t = 1 - t
        upto = self.tiles[t][:, 4:]
        link(v.tensor_tensor(self.base[:, :], upto, self.ntile[:, :], ALU.subtract))
        link(v.tensor_tensor(A(self.slot), cum[:, 8:, :], A(self.tot), ALU.subtract))
        link(v.tensor_tensor(A(self.slot), A(self.slot), A(self.pre), ALU.add))
        link(v.scalar_tensor_tensor(out=A(self.slot), in0=self.base[:, :].unsqueeze(1).to_broadcast([P, NT, E]),
                                    scalar=float(P), in1=A(self.slot), op0=ALU.mult, op1=ALU.add))
        for b, oh in enumerate((self.oh1, self.oh2)):
            link(v.tensor_tensor(A(self.L2), A(self.slot), A(oh), ALU.mult))
            link(v.tensor_reduce(out=self.sf[b][:, :], in_=A(self.L2), axis=AX.X, op=ALU.add))
            v.tensor_copy(self.si[b][:, :], self.sf[b][:, :]).then_inc(self.slots_ok, 1)
        dve.wait_ge(p3_ok, 2 * NC)
        link(v.tensor_tensor(self.tcmp[:, :, :], self.tau[:, :].unsqueeze(2).to_broadcast([P, MT, E - 1]),
                             upto[:, 0:E - 1].unsqueeze(1).to_broadcast([P, MT, E - 1]), ALU.is_ge))
        link(v.tensor_reduce(out=self.texp[:, :], in_=self.tcmp[:, :, :], axis=AX.X, op=ALU.add))
        v.tensor_copy(self.tile_expert[:, :], self.texp[:, :])
        v.tensor_scalar(self.tile_cols[:, :], self.texp[:, :], float(F), None, ALU.mult).then_inc(self.slots_ok, 1)

    def pool_slots(self, pool):
        pool.wait_ge(self.slots_ok, 3)
        pool.wait_ge(self.filled, 16)

    def scatter(self, pool, xn, slot_x, n):
        i, b = n // 2, n % 2
        pool.indirect_dma_start(
            out=slot_x, out_offset=bass.IndirectOffsetOnAxis(ap=self.si[b][:, i:i + 1].bitcast(U32), axis=0),
            in_=xn[:, i, :], in_offset=None).then_inc(self.scattered, 16)


class Ffn:

    STEPS = MT + 3
    FIRST, BODY = 6, 6
    EARLY = 2
    AHEAD = 2

    def __init__(self, nc, sb, sem, probs, route, weights, places):
        self.nc = nc
        self.route = route
        self.weights = [w[:, :] for w in weights[0:2]]
        self.W2 = weights[2]
        self.high = [a.bitcast(F32R) for a in places]
        self.low = [w.bitcast(F32R) for w in self.weights]
        self.places = places
        self.xg = sb("ff_xg", [P, 3, D])
        self.xT_high = sb("ff_xT", [P, 2, P])[:, :, :].bitcast(F32R)
        self.xT_low = sb("ff_xT_low", [P, 2, P])[:, :, :].bitcast(F32R)
        self.sg = probs[:, 0:2, :]
        self.hh = probs[:, 2:4, :]
        self.hT = probs[:, 4:6, :]
        self.y = sb("ff_y", [P, 3, D])
        self.x_in = [sem(f"ff_x_in{u}") for u in range(3)]
        self.y_out = [sem(f"ff_y_out{u}") for u in range(3)]
        self.w_high = sem("ff_w_high")
        self.w_low = sem("ff_w_low")
        self.w_ok = sem("ff_w_ok")
        self.t_mm = sem("ff_t_mm")
        self.t_high = sem("ff_t_high")
        self.t_ok = sem("ff_t_ok")
        self.u1_mm = sem("ff_u1_mm")
        self.u3_mm = sem("ff_u3_mm")
        self.g_ok = sem("ff_g_ok")
        self.h_ok = sem("ff_h_ok")
        self.ht_mm = sem("ff_ht_mm")
        self.ht_ok = sem("ff_ht_ok")
        self.y_mm = sem("ff_y_mm")
        self.y_ok = sem("ff_y_ok")

    def act_split(self, act):
        for e in range(E):
            for w in range(2):
                cols = slice(e * F, (e + 1) * F)
                self.nc.scalar.activation(self.high[w][:, cols], self.weights[w][:, cols], ACT.Copy
                                          ).then_inc(self.w_high, 1)

    def pool_split(self, pool):
        for e in range(E):
            for w in range(2):
                cols = slice(e * F, (e + 1) * F)
                pool.wait_ge(self.w_high, 2 * e + w + 1)
                self.nc.gpsimd.tensor_tensor(self.low[w][:, cols], self.weights[w][:, cols],
                                             self.places[w][:, cols], ALU.subtract
                                             ).then_inc(self.w_ok if w else self.w_low, 1)

    def early(self, step):
        for s in range(self.EARLY):
            step(s, s, s // 3)

    def turned(self, s, psM, psO):
        return psO[:, s * P:(s + 1) * P] if isinstance(s, int) and s <= self.EARLY else psM[:, 2, 0:P]

    def steps(self, eng, step, before_loop=None, first=EARLY):
        for s in range(first, self.FIRST):
            step(s, s, s // 3)
        n = (MT - self.AHEAD - self.FIRST) // self.BODY
        rest = self.FIRST + n * self.BODY
        if before_loop:
            before_loop()
        with eng.Fori(0, n) as it:
            for v in range(self.BODY):
                step(it * self.BODY + (self.FIRST + v), self.FIRST + v, it * 2 + (self.FIRST + v) // 3)
        for s in range(rest, self.STEPS):
            step(s, s, s // 3)

    @staticmethod
    def live(s, lag):
        return not isinstance(s, int) or 0 <= s - lag < MT

    @staticmethod
    def wait(eng, sem, value):
        if not isinstance(value, int) or value > 0:
            eng.wait_ge(sem, value)

    def sp_first(self, sp, slot_x, route):
        sp.wait_ge(route.scattered, 16 * 2 * NT)
        for s in range(3):
            sp.dma_start(self.xg[:, s, :], slot_x[s * P:(s + 1) * P, :]).then_inc(self.x_in[s], 16)

    def sp(self, sp, slot_x, slot_y, first_stacks):
        def load(s, v, k):
            if isinstance(s, int):
                if s < 3 or s >= MT:
                    return
                sp.wait_ge(self.t_mm, s - 2)
                src = slot_x[s * P:(s + 1) * P, :]
            else:
                sp.wait_ge(self.t_mm, s - 2)
                src = slot_x[bass.ds(s * P, P), :]
            sp.dma_start(self.xg[:, v % 3, :], src).then_inc(self.x_in[v % 3], 16)

        def step(s, v, k):
            if isinstance(s, int) and s == MT:
                sp.wait_ge(self.u3_mm, MT)
                first_stacks()
            load(s + self.AHEAD, v + self.AHEAD, k)
            if self.live(s, 3):
                sp.wait_ge(self.y_ok, s - 2)
                dst = slot_y[(s - 3) * P:(s - 2) * P, :] if isinstance(s, int) else slot_y[bass.ds((s - 3) * P, P), :]
                sp.dma_start(dst, self.y[:, v % 3, :]).then_inc(self.y_out[v % 3], 16)

        self.steps(sp, step, first=0)

    def pe_step(self, pe, ident, psS, psM, psO):
        nc = self.nc
        columns = {}

        def first_column(tau):
            at = self.route.tile_cols
            at = at[0:1, tau:tau + 1] if isinstance(tau, int) else at[0:1, bass.ds(tau, 1)]
            return nc.values_load(at, engines=[mybir.EngineType.PE], min_val=0, max_val=(E - 1) * F,
                                  skip_runtime_bounds_check_because="F times a count of seven comparisons")

        def three_passes(dst, high, low, w, first):
            cols = bass.ds(first, F)
            nc.tensor.matmul(dst, high, self.high[w][:, cols], start=True, stop=False)
            nc.tensor.matmul(dst, high, self.low[w][:, cols], start=False, stop=False)
            return nc.tensor.matmul(dst, low, self.high[w][:, cols], start=False, stop=True)

        def step(s, v, k):
            if not isinstance(s, int) and v == self.FIRST:
                columns.clear()
            if self.live(s, 0):
                pe.wait_ge(self.x_in[v % 3], k * 16 + 16)
                self.wait(pe, self.t_ok, s)
                nc.tensor.transpose(self.turned(s, psM, psO), self.xg[:, v % 3, :], ident[:, :]).then_inc(self.t_mm, 1)
            if self.live(s, 1):
                b = (v - 1) % 2
                first = columns[v - 1] = first_column(s - 1)
                if isinstance(s, int) and s < self.FIRST:
                    tau = self.route.tile_expert[0:1, s - 1:s]
                    pe.wait_ge(self.w_ok, pe.value_load(tau, min_val=0, max_val=E - 1) + 1)
                pe.wait_ge(self.t_ok, s)
                self.wait(pe, self.h_ok, s - 2)
                for w, done in ((0, self.u1_mm), (1, self.u3_mm)):
                    three_passes(psS[:, 2 * b + w, :], self.xT_high[:, b, :], self.xT_low[:, b, :], w, first
                                 ).then_inc(done, 1)
            if self.live(s, 2):
                b = (v - 2) % 2
                pe.wait_ge(self.h_ok, s - 1)
                self.wait(pe, self.ht_ok, s - 3)
                if isinstance(s, int) and s == self.EARLY:
                    pe.wait_ge(self.m_red, NF)
                for c in range(FC):
                    last = nc.tensor.transpose(psM[:, b, c * P:(c + 1) * P], self.hh[:, b, c * P:(c + 1) * P],
                                               ident[:, :])
                last.then_inc(self.ht_mm, 1)
            if self.live(s, 3):
                b = (v - 3) % 2
                first = columns.pop(v - 3) if v - 3 in columns else first_column(s - 3)
                pe.wait_ge(self.ht_ok, s - 2)
                self.wait(pe, self.y_ok, s - 3)
                for c in range(FC):
                    last = nc.tensor.matmul(psO[:, 0:D], self.hT[:, b, c * P:(c + 1) * P],
                                            self.W2[:, c * D:][:, bass.ds(first, D)], start=(c == 0), stop=(c == FC - 1))
                last.then_inc(self.y_mm, 1)

        return step

    def pe_end(self, pe):
        pe.wait_ge(self.h_ok, MT)
        pe.wait_ge(self.y_ok, MT)

    def dve_step(self, dve, link, psS, psM, psO):
        nc = self.nc

        def step(s, v, k):
            if self.live(s, 0):
                dve.wait_ge(self.t_high, s + 1)
                nc.vector.tensor_tensor(self.xT_low[:, v % 2, :], self.turned(s, psM, psO),
                                        self.xT_high[:, v % 2, :].bitcast(F32), ALU.subtract).then_inc(self.t_ok, 1)
            if self.live(s, 1):
                b = (v - 1) % 2
                dve.wait_ge(self.g_ok, s)
                dve.wait_ge(self.u3_mm, s)
                self.wait(dve, self.ht_mm, s - 2)
                nc.vector.tensor_tensor(self.hh[:, b, :], self.sg[:, b, :], psS[:, 2 * b + 1, :],
                                        ALU.mult).then_inc(self.h_ok, 1)
            if self.live(s, 3):
                dve.wait_ge(self.y_mm, s - 2)
                if isinstance(s, int):
                    self.wait(dve, self.y_out[v % 3], 16 * (k - 1))
                else:
                    dve.wait_ge(self.y_out[v % 3], k * 16 - 16)
                nc.vector.tensor_copy(self.y[:, v % 3, :], psO[:, 0:D]).then_inc(self.y_ok, 1)
            if isinstance(s, int) and s == 3:
                self.route.dve_weight1(dve, link)
            if isinstance(s, int) and s == 4:
                self.route.dve_weight2(dve, link)

        return step

    def act_step(self, act, psS, psM, psO):
        nc = self.nc

        def step(s, v, k):
            if self.live(s, 0):
                act.wait_ge(self.t_mm, s + 1)
                self.wait(act, self.u3_mm, s - 1)
                nc.scalar.activation(self.xT_high[:, v % 2, :], self.turned(s, psM, psO), ACT.Copy).then_inc(self.t_high, 1)
            if self.live(s, 1):
                b = (v - 1) % 2
                act.wait_ge(self.u1_mm, s)
                self.wait(act, self.h_ok, s - 2)
                nc.scalar.activation(self.sg[:, b, :], psS[:, 2 * b, :], ACT.Silu).then_inc(self.g_ok, 1)
            if self.live(s, 2):
                b = (v - 2) % 2
                act.wait_ge(self.ht_mm, s - 1)
                self.wait(act, self.y_mm, s - 3)
                nc.scalar.activation(self.hT[:, b, :], psM[:, b, :], ACT.Copy).then_inc(self.ht_ok, 1)

        return step

    def pool(self, pool):
        for u in range(3):
            pool.wait_ge(self.y_out[u], 16 * (MT // 3))


class Final:

    BEFORE = (NG - 1) * HG
    ROWS = BEFORE * DK

    def __init__(self, nc, sem, W1, W3, W2, Vp, orow, wo_sb, wo_last, take_den, rest):
        self.nc = nc
        tiled = [w[:, b * T:(b + 1) * T].rearrange("p (i d) -> p i d", d=D) for w in (W1, W3) for b in range(2)]
        self.rows = tiled[0:2]
        self.gate = tiled[2]
        self.res = tiled[3]
        self.orow, self.wo_sb, self.wo_last, self.take_den, self.rest = orow, wo_sb, wo_last, take_den, rest
        flat = Vp[:, :, :, :].rearrange("p i h w -> p (i h w)")
        self.num, self.rec = (flat[:, b * T:(b + 1) * T] for b in range(2))
        self.den = W2[0:self.ROWS, 0:T // DK]
        self.rows_in = sem("fn_rows_in")
        self.weighted = sem("fn_weighted")
        self.mix_ok = sem("fn_mix_ok")
        self.left_zero = sem("fn_left_zero")
        self.gate_exp = sem("fn_gate_exp")
        self.gate_den = sem("fn_gate_den")
        self.gate_rec = sem("fn_gate_rec")
        self.gate_ok = sem("fn_gate_ok")
        self.wo_in = sem("fn_wo_in")
        self.num_in = sem("fn_num_in")
        self.den_in = sem("fn_den_in")
        self.rec_ok = sem("fn_rec_ok")
        self.rec_out = sem("fn_rec_out")
        self.rec_in = sem("fn_rec_in")
        self.den_ps = sem("fn_den_ps")
        self.attn_ok = sem("fn_attn_ok")
        self.proj_mm = sem("fn_proj_mm")
        self.res_ok = sem("fn_res_ok")
        self.out_ok = sem("fn_out_ok")

    def gather(self, pool, route, slot_y, n):
        i, b = n // 2, n % 2
        pool.indirect_dma_start(
            out=self.rows[b][:, i, :], out_offset=None, in_=slot_y,
            in_offset=bass.IndirectOffsetOnAxis(ap=route.si[b][:, i:i + 1].bitcast(U32), axis=0),
        ).then_inc(self.rows_in, 16)

    def sp_weights(self, sp, woT):
        for h in range(HG):
            r = self.ROWS + h * DK
            sp.dma_start(self.wo_last[32 * h:32 * h + DK, :], woT[r:r + DK, :]).then_inc(self.wo_in, 16)

    def sp_sums(self, sp, attn_raw):
        heads = attn_raw.rearrange("g (h r) n -> (g h) r n", r=32)
        sp.dma_start(self.den[:, :], heads[:, DK, :].rearrange("h (q n) -> h q n", q=DK)).then_inc(self.den_in, 16)
        sp.dma_start(self.num[0:self.ROWS, :], heads[:, 0:DK, :]).then_inc(self.num_in, 16)

    def sp_recips(self, sp, recips):
        sp.wait_ge(self.rec_ok, 1)
        sp.dma_start(recips.rearrange("h (q n) -> (h q) n", q=DK), self.den[:, :]).then_inc(self.rec_out, 16)
        sp.wait_ge(self.rec_out, 16)
        sp.dma_start(self.rec[0:self.ROWS, :],
                     recips.unsqueeze(1).to_broadcast([self.BEFORE, DK, T])).then_inc(self.rec_in, 16)

    def sp_out(self, sp, out):
        for k, (c, first, end) in enumerate(PIECES):
            sp.wait_ge(self.res_ok, k + 1)
            sp.dma_start(out[c * CW + first:c * CW + end, :].rearrange("(i p) d -> p i d", p=P),
                         self.res[:, c * TC + first // P:c * TC + end // P, :]).then_inc(self.out_ok, 16)
        sp.wait_ge(self.out_ok, 16 * NPC)


    @staticmethod
    def chunk(k):
        return slice(k * TC, (k + 1) * TC)

    def act(self, act, k):
        if k == 0:
            act.wait_ge(self.mix_ok, 1)
        self.nc.scalar.activation(self.rows[0][:, self.chunk(k), :], self.gate[:, self.chunk(k), :], ACT.Exp,
                                  scale=-1.0).then_inc(self.gate_exp, 1)

    def pool_gate_den(self, pool):
        for k in range(NC):
            e = self.rows[0][:, self.chunk(k), :]
            pool.wait_ge(self.gate_exp, k + 1)
            self.nc.gpsimd.tensor_scalar(e, e, 1.0, None, ALU.add).then_inc(self.gate_den, 1)

    def pool_gate(self, pool):
        for k in range(NC):
            y = self.gate[:, self.chunk(k), :]
            pool.wait_ge(self.gate_rec, k + 1)
            self.nc.gpsimd.tensor_tensor(y, y, self.rows[0][:, self.chunk(k), :], ALU.mult).then_inc(self.gate_ok, 1)

    def pool_mix(self, pool, route):
        nc = self.nc
        pool.wait_ge(self.rows_in, 16 * 2 * NT)
        for b, w in enumerate((route.w1, route.w2)):
            nc.gpsimd.tensor_tensor(self.rows[b], self.rows[b], w[:, :].unsqueeze(2).to_broadcast([P, NT, D]),
                                    ALU.mult).then_inc(self.weighted, 1)
        pool.wait_ge(self.weighted, 2)
        nc.gpsimd.tensor_tensor(self.gate, self.rows[0], self.rows[1], ALU.add).then_inc(self.mix_ok, 1)

    def dve(self, dve, link, psM, psS, X):
        nc = self.nc

        def normalise(k):
            c, first, end = PIECES[k]
            rec = self.rest[:, k % 2, 0:end - first]
            view = self.orow[:, c, first:end]
            dve.wait_ge(self.den_ps, k + 1)
            link(nc.vector.reciprocal(rec, self.spread_place(psM, k)))
            nc.vector.tensor_tensor(view, view, rec, ALU.mult).then_inc(self.attn_ok, 1)

        def residual(k):
            c, first, end = PIECES[k]
            tiles = slice(c * TC + first // P, c * TC + end // P)
            dve.wait_ge(self.gate_ok, c + 1)
            dve.wait_ge(self.proj_mm, k + 1)
            link(nc.vector.tensor_tensor(self.res[:, tiles, :], self.gate[:, tiles, :],
                                         self.project_bank(psM, psS, k)[:, 0:end - first].rearrange("p (i d) -> p i d", d=D), ALU.mult))
            nc.vector.tensor_tensor(self.res[:, tiles, :], self.res[:, tiles, :], X[:, tiles, :],
                                    ALU.add).then_inc(self.res_ok, 1)

        def gate_reciprocal(k):
            e = self.rows[0][:, self.chunk(k), :]
            dve.wait_ge(self.gate_den, k + 1)
            nc.vector.reciprocal(e, e).then_inc(self.gate_rec, 1)

        nc.vector.memset(psM[:, 1, 0:CW // 2], 0.0).then_inc(self.left_zero, 1)
        dve.wait_ge(self.den_in, 16)
        nc.vector.reciprocal(self.den[:, :], self.den[:, :]).then_inc(self.rec_ok, 1)
        normalise(0)
        dve.wait_ge(self.num_in, 16)
        dve.wait_ge(self.rec_in, 16)
        nc.vector.tensor_tensor(self.num[0:self.ROWS, :], self.num[0:self.ROWS, :], self.rec[0:self.ROWS, :],
                                ALU.mult).then_inc(self.attn_ok, 1)
        gate_reciprocal(0)
        gate_reciprocal(1)
        normalise(1)
        residual(0)
        gate_reciprocal(2)
        gate_reciprocal(3)
        normalise(2)
        residual(1)
        residual(2)
        normalise(3)
        normalise(4)
        residual(3)
        residual(4)

    @staticmethod
    def spread_place(psM, k):
        _, first, end = PIECES[k]
        return psM[:, 0, 0:end - first] if k < NPC - 1 else psM[:, 1, first:end]

    def spread(self, pe, k, psM, o_row):
        c, first, end = PIECES[k]
        pe.wait_ge(o_row, (NG - 1) * NC + k + 2)
        if k:
            pe.wait_ge(self.attn_ok, (0, 1, 3, 4, 4)[k])
        else:
            pe.wait_ge(self.m_red, NF + (NG - 1) * NI + NL)
        self.nc.tensor.matmul(self.spread_place(psM, k), self.take_den[:, :], self.orow[:, c, first:end],
                              start=True, stop=True).then_inc(self.den_ps, 1)

    @staticmethod
    def project_bank(psM, psS, k):
        return psM[:, 2, :] if k < NPC - 1 else psS[:, 0, :]

    def project(self, pe, k, psM, psS):
        c, first, end = PIECES[k]
        pe.wait_ge(self.wo_in, 16 * HG)
        pe.wait_ge(self.attn_ok, k + 2)
        if 0 < k < NPC - 1:
            pe.wait_ge(self.res_ok, k)
        for i in range((end - first) // P):
            t0 = c * CW + first + i * P
            dst = self.project_bank(psM, psS, k)[:, i * D:(i + 1) * D]
            self.nc.tensor.matmul(dst, self.num[0:self.ROWS, t0:t0 + P], self.wo_sb[0:self.ROWS, :],
                                  start=True, stop=False)
            last = self.nc.tensor.matmul(dst, self.orow[:, c, first + i * P:first + (i + 1) * P], self.wo_last[:, :],
                                         start=False, stop=True)
        last.then_inc(self.proj_mm, 1)


def kernel(L0_attn_x, L0_attn_w_qkv, L0_attn_w_o, L0_ffn_gate_w, L0_ffn_w1, L0_ffn_w2, L0_ffn_w3):
    import numpy as np
    import concourse.bacc as bacc
    from concourse.bass_utils import run_bass_kernel_spmd

    def flat(a, *axes):
        a = np.asarray(a)
        return np.ascontiguousarray(a.transpose(*axes) if axes else a)

    w = flat(L0_attn_w_qkv)
    w_rows = np.concatenate([w[0:2].transpose(0, 2, 1, 3).reshape(2 * D, D), w[2].reshape(D, D)])
    arrays = {
        "x": flat(L0_attn_x).reshape(T, D),
        "wqkvT": flat(w_rows, 1, 0),
        "woT": flat(L0_attn_w_o, 1, 0),
        "gateT": flat(L0_ffn_gate_w, 1, 0),
        "w1T": flat(L0_ffn_w1, 0, 2, 1),
        "w3T": flat(L0_ffn_w3, 0, 2, 1),
        "w2T": flat(L0_ffn_w2, 0, 2, 1),
    }
    nc = bacc.Bacc("TRN2", target_bir_lowering=False, num_devices=1)
    args = {n: nc.dram_tensor(n, a.shape, F32, kind="ExternalInput").ap() for n, a in arrays.items()}
    args["out"] = nc.dram_tensor("out", (T, D), F32, kind="ExternalOutput").ap()
    build(nc, **args)
    r = run_bass_kernel_spmd(nc, [arrays], core_ids=[0])
    return r.results[0]["out"].reshape(1, T, D)
```
